# Optimizing a Trainium2 kernel written in Bass

```python
import numpy as np
import jax
import jax.numpy as jnp

def _softmax(x, axis=-1):
    return jax.nn.softmax(x, axis=axis)

def _gelu(x):
    return jax.nn.gelu(x, approximate=True)

def _silu(x):
    return jax.nn.silu(x)

def _sigmoid(x):
    return jax.nn.sigmoid(x)

def _layernorm(x, axis=-1, eps=1e-05):
    m = jnp.mean(x, axis=axis, keepdims=True)
    v = jnp.var(x, axis=axis, keepdims=True)
    return (x - m) / jnp.sqrt(v + eps)

def _scatter_add(tgt, idx, src, axis=0):
    return tgt.at[idx].add(src)

def _segment_sum(src, seg, n):
    return jax.ops.segment_sum(src, seg, n)
kernel_name = 'mk_prb_d1_jaxref_r4_c64dc7'

def setup_inputs(seed: int=0):
    np.random.seed(seed)
    _w = jnp.asarray

    def _L0_attn_setup():
        import jax, jax.numpy as jnp
        import numpy as np
        DIM = 256
        EPS = 1e-05

        def _layernorm(x, w, b):
            mu = jnp.mean(x, axis=-1, keepdims=True)
            var = jnp.mean(jnp.square(x - mu), axis=-1, keepdims=True)
            return (x - mu) * jax.lax.rsqrt(var + EPS) * w + b
        key = jax.random.key(seed)
        ks = jax.random.split(key, 7)
        C = DIM
        x = jax.random.normal(ks[0], (4, 1024, C), dtype=jnp.float32)
        norm_w = jnp.ones((C,), dtype=jnp.float32)
        norm_b = jnp.zeros((C,), dtype=jnp.float32)
        s = 1.0 / np.sqrt(C)
        qkv_w = jax.random.uniform(ks[1], (3 * C, C), dtype=jnp.float32, minval=-s, maxval=s)
        qkv_b = jax.random.uniform(ks[2], (3 * C,), dtype=jnp.float32, minval=-s, maxval=s)
        proj_w = jax.random.uniform(ks[3], (C, C), dtype=jnp.float32, minval=-s, maxval=s)
        proj_b = jax.random.uniform(ks[4], (C,), dtype=jnp.float32, minval=-s, maxval=s)
        return {'x': x, 'norm_w': norm_w, 'norm_b': norm_b, 'qkv_w': qkv_w, 'qkv_b': qkv_b, 'proj_w': proj_w, 'proj_b': proj_b}
    _L0_attn_in = _L0_attn_setup()

    def _L0_ffn_setup():
        import jax, jax.numpy as jnp
        import numpy as np
        B, S, D, H, E = (8, 512, 256, 1024, 16)
        key = jax.random.key(seed)
        ks = jax.random.split(key, 4)
        sd = 1.0 / np.sqrt(D).astype(np.float32)
        sh = 1.0 / np.sqrt(H).astype(np.float32)
        return {'x': jax.random.normal(ks[0], (B, S, D), jnp.float32), 'Wg': jax.random.normal(ks[1], (D, E), jnp.float32) * sd, 'bg': jnp.zeros((E,), jnp.float32), 'W1': jax.random.normal(ks[2], (E, D, H), jnp.float32) * sd, 'b1': jnp.zeros((E, H), jnp.float32), 'W2': jax.random.normal(ks[3], (E, H, D), jnp.float32) * sh, 'b2': jnp.zeros((E, D), jnp.float32)}
    _L0_ffn_in = _L0_ffn_setup()
    _d = {'L0_attn_x': _L0_attn_in['x'], 'L0_attn_norm_w': _L0_attn_in['norm_w'], 'L0_attn_norm_b': _L0_attn_in['norm_b'], 'L0_attn_qkv_w': _L0_attn_in['qkv_w'], 'L0_attn_qkv_b': _L0_attn_in['qkv_b'], 'L0_attn_proj_w': _L0_attn_in['proj_w'], 'L0_attn_proj_b': _L0_attn_in['proj_b'], 'L0_ffn_Wg': _L0_ffn_in['Wg'], 'L0_ffn_bg': _L0_ffn_in['bg'], 'L0_ffn_W1': _L0_ffn_in['W1'], 'L0_ffn_b1': _L0_ffn_in['b1'], 'L0_ffn_W2': _L0_ffn_in['W2'], 'L0_ffn_b2': _L0_ffn_in['b2']}
    _x0 = _d['L0_attn_x']
    _d['L0_attn_x'] = jax.random.normal(jax.random.fold_in(jax.random.key(seed), 1), (4, 2048, 256), dtype=_x0.dtype)
    del _x0
    return _d

def reference(L0_attn_x, L0_attn_norm_w, L0_attn_norm_b, L0_attn_qkv_w, L0_attn_qkv_b, L0_attn_proj_w, L0_attn_proj_b, L0_ffn_Wg, L0_ffn_bg, L0_ffn_W1, L0_ffn_b1, L0_ffn_W2, L0_ffn_b2):

    def _L0_attn_ref(x, norm_w, norm_b, qkv_w, qkv_b, proj_w, proj_b):
        import jax, jax.numpy as jnp
        import numpy as np
        DIM = 256
        EPS = 1e-05

        def _layernorm(x, w, b):
            mu = jnp.mean(x, axis=-1, keepdims=True)
            var = jnp.mean(jnp.square(x - mu), axis=-1, keepdims=True)
            return (x - mu) * jax.lax.rsqrt(var + EPS) * w + b
        B, T, C = x.shape
        residual = x
        h = _layernorm(x, norm_w, norm_b)
        qkv = jnp.einsum('btc,oc->bto', h, qkv_w) + qkv_b
        q, k, v = (qkv[..., :C], qkv[..., C:2 * C], qkv[..., 2 * C:])
        attn = jnp.einsum('btc,bsc->bts', q, k) / jnp.sqrt(jnp.float32(C))
        o = jnp.einsum('bts,bsc->btc', attn, v)
        o = jnp.einsum('btc,oc->bto', o, proj_w) + proj_b
        return residual + o

    def _L0_ffn_ref(x, Wg, bg, W1, b1, W2, b2):
        import jax, jax.numpy as jnp
        import numpy as np
        B, S, D, H, E = (8, 512, 256, 1024, 16)
        d = x.shape[-1]
        xf = x.reshape(-1, d)
        n_tok = xf.shape[0]
        n_exp = Wg.shape[1]
        cap = -(-n_tok // n_exp)
        score = jax.nn.softmax(xf @ Wg + bg, axis=-1)
        gate = jnp.max(score, axis=-1)
        idx = jnp.argmax(score, axis=-1)
        onehot = jax.nn.one_hot(idx, n_exp, dtype=jnp.int32)
        pos = jnp.sum((jnp.cumsum(onehot, axis=0) - 1) * onehot, axis=-1)
        keep = pos < cap
        safe_pos = jnp.where(keep, pos, cap - 1)
        buf = jnp.zeros((n_exp, cap, d), x.dtype).at[idx, safe_pos].add(jnp.where(keep[:, None], xf, 0.0))
        h = jax.nn.relu(jnp.einsum('ecd,edh->ech', buf, W1) + b1[:, None, :])
        y = jnp.einsum('ech,ehd->ecd', h, W2) + b2[:, None, :]
        out = y[idx, safe_pos] * gate[:, None]
        out = jnp.where(keep[:, None], out, 0.0)
        return out.reshape(x.shape)
    x = L0_attn_x
    xn = _layernorm(x, axis=-1)
    x = x + _L0_attn_ref(xn, L0_attn_norm_w, L0_attn_norm_b, L0_attn_qkv_w, L0_attn_qkv_b, L0_attn_proj_w, L0_attn_proj_b) + _L0_ffn_ref(xn, L0_ffn_Wg, L0_ffn_bg, L0_ffn_W1, L0_ffn_b1, L0_ffn_W2, L0_ffn_b2)
    return x

_drawn_inputs = setup_inputs


def setup_inputs(seed=0):
    import zlib

    import numpy as np

    out = dict(_drawn_inputs(seed))
    spreads = {'L0_attn_norm_w': (1.0, 0.2),
     'L0_attn_norm_b': (0.0, 0.1),
     'L0_ffn_bg': (0.0, 0.8),
     'L0_ffn_b1': (0.0, 0.8),
     'L0_ffn_b2': (0.0, 2.0)}
    factors = {'L0_attn_proj_b': 50.537, 'L0_ffn_Wg': 6.164, 'L0_ffn_W1': 7.359, 'L0_ffn_W2': 6.08}
    for name, (base, spread) in spreads.items():
        noise = np.random.default_rng([zlib.crc32(name.encode()), seed]).standard_normal(out[name].shape)
        drawn = base * np.exp(spread * noise) if base else spread * noise
        out[name] = jnp.asarray(drawn.astype(out[name].dtype))
    for name, factor in factors.items():
        out[name] = (out[name] * factor).astype(out[name].dtype)
    return out
```

```python
from contextlib import ExitStack

import concourse.bass as bass
from concourse import mybir
from concourse.alu_op_type import AluOpType as ALU

ACT = mybir.ActivationFunctionType
F32 = mybir.dt.float32
U32 = mybir.dt.uint32
AX = mybir.AxisListType.X

P = 128
NB = 4
T = 2048
C = 256
KC = C // P
J = T // P
PAIRS = J // 2
E = 16
H = 1024
HC = H // P
NTOK = NB * T
CAP = -(-NTOK // E)
S = CAP // P
EPS = 1e-5
ZW = C + 2
SKIP = 2.0 * NTOK
META = 4


def program(nc, x, norm_w, norm_b, qkv_w, qkv_b, proj_w, proj_b, Wg, bg, W1, b1, W2, b2, out):
    table = nc.dram_tensor("slot_records", (E * CAP, META), F32).ap()
    xrows = x.rearrange("b t c -> (b t) c")
    orows = out.rearrange("b t c -> (b t) c")
    xb = x.rearrange("b (p j) c -> b p j c", j=J)
    ob = out.rearrange("b (p j) c -> b p j c", j=J)

    with ExitStack() as ctx:
        def sb(name, shape, dt=F32, stack=None):
            return (stack or ctx).enter_context(nc.sbuf_tensor(name, shape, dt))

        def sem(name):
            return ctx.enter_context(nc.semaphore(name))

        def two(name, shape, dt=F32, stack=None):
            return [sb(f"{name}{q}", shape, dt, stack) for q in range(2)]

        bank = [ctx.enter_context(nc.psum_tensor(f"bank{n}", [P, 512], F32)) for n in range(8)]
        tr_ps, g_ps, lg_ps, o_ps = bank[0:2], bank[2:4], bank[4:6], bank[6:8]
        h_ps, y_ps, xt_ps = bank[0:4], bank[4:6], bank[6:8]

        ident = sb("ident", [P, P])
        tri = sb("tri", [P, P])
        ones = sb("ones", [P, P])
        zeros = sb("zeros", [P, E * CAP * META // P])
        scan_mask = sb("scan_mask", [P, E, J])
        rev = sb("rev", [P, E])
        token1 = sb("token1", [P, NB * J])
        wqkv = sb("wqkv", [P, 6, ZW])
        wp = sb("wp", [P, KC, C])
        wpT = sb("wpT", [P, KC, C])
        nw = sb("nw", [P, C])
        nb_ = sb("nb", [P, C])
        dots = sb("dots", [P, 6])
        qkvb = sb("qkvb", [P, 6])
        bp = sb("bp", [P, C])
        AT = sb("AT", [P, KC, C + 1])
        Acol = sb("Acol", [P, KC])
        Alast = sb("Alast", [P, 1])
        Bm = sb("Bm", [P, KC, C])
        Blast = sb("Blast", [P, C])
        Bsum = sb("Bsum", [P, C])
        wg = sb("wg", [P, KC, E])
        bgb = sb("bgb", [P, E])
        b1rows = sb("b1rows", [P, P])
        b1T = sb("b1T", [P, E * HC])
        G = sb("G", [P, KC, C + 1])
        Tm = sb("Tm", [P, KC, C])
        Tlast = sb("Tlast", [P, C])
        M = two("M", [P, KC, C])
        cb = two("cb", [P, C])
        st = sb("st", [P, J, 6])
        s1 = sb("s1", [P, 8, J])
        stds = two("stds", [P, 2, J])
        var2 = two("var2", [P, 2, J])
        mean = two("mean", [P, J])
        rstd = two("rstd", [P, 2, J])
        s2 = two("s2", [P, J])
        rp1 = two("rp1", [P, J])
        nmr = two("nmr", [P, J])
        L = sb("L", [P, J, E])
        D = sb("D", [P, J, E])
        Ex = sb("Ex", [P, J, E])
        key = sb("key", [P, J, E])
        onehot = sb("onehot", [P, E, J])
        count = sb("count", [P, E, J])
        posm = sb("posm", [P, E, J])
        r1 = sb("r1", [P, 8, J])
        total = two("total", [P, E])
        dst = two("dst", [P, J], U32)
        meta = two("meta", [P, J, META])
        w1 = two("w1", [P, KC, H])
        w2 = two("w2", [P, HC, C])
        b2b = two("b2b", [P, C])
        rec = sb("rec", [P, E * S * META])
        idf = sb("idf", [P, 2, E * S])
        ids = sb("ids", [P, E * S], U32)
        idx_x = two("idx_x", [P, S], U32)
        idx_o = two("idx_o", [P, S], U32)
        gate = sb("gate", [P, 2])

        early = ctx.enter_context(ExitStack())
        xs = two("xs", [P, J, C], stack=early)
        z = two("z", [P, J, ZW], stack=early)
        zT = two("zT", [P, KC, T], stack=early)
        osb = [t[:, :, 0:C] for t in z]
        early.close()
        late = ctx.enter_context(ExitStack())
        xg = two("xg", [P, S, C], stack=late)
        xn = two("xn", [P, S, C], stack=late)
        res = two("res", [P, S, C], stack=late)
        xnT = sb("xnT", [P, KC, CAP], stack=late)
        hT = sb("hT", [P, HC, CAP], stack=late)

        consts_made = sem("consts_made")
        attn_w_loaded = sem("attn_w_loaded")
        router_w_loaded = sem("router_w_loaded")
        x_loaded = [[sem(f"x_loaded{q}{h}") for h in range(2)] for q in range(2)]
        table_zeroed = sem("table_zeroed")
        w_loaded = [sem(f"w_loaded{q}") for q in range(2)]
        b1_loaded = sem("b1_loaded")
        setup_pe = sem("setup_pe")
        setup_dve = sem("setup_dve")
        dve_chain = sem("dve_chain")
        var_ready = sem("var_ready")
        std_ready = sem("std_ready")
        z_ready = sem("z_ready")
        tr_done = sem("tr_done")
        zT_ready = sem("zT_ready")
        g_done = sem("g_done")
        g_saved = sem("g_saved")
        logits_done = sem("logits_done")
        shifted_ready = sem("shifted_ready")
        exp_ready = sem("exp_ready")
        count_ready = sem("count_ready")
        prefix_done = sem("prefix_done")
        chain_done = sem("chain_done")
        chain_saved = sem("chain_saved")
        meta_ready = sem("meta_ready")
        meta_scattered = [sem(f"meta_scattered{q}") for q in range(2)]
        o_done = sem("o_done")
        o_summed = sem("o_summed")
        o_stored = [sem(f"o_stored{q}") for q in range(2)]
        rec_loaded = sem("rec_loaded")
        ids_ready = sem("ids_ready")
        idx_copied = sem("idx_copied")
        gate_passed = sem("gate_passed")
        xg_loaded = [sem(f"xg_loaded{q}") for q in range(2)]
        res_loaded = [sem(f"res_loaded{q}") for q in range(2)]
        xn_ready = sem("xn_ready")
        xt_done = sem("xt_done")
        xnT_ready = sem("xnT_ready")
        h_done = sem("h_done")
        h_act = sem("h_act")
        h_dve = sem("h_dve")
        y_done = sem("y_done")
        y_free = sem("y_free")
        res_ready = sem("res_ready")
        res_stored = [sem(f"res_stored{q}") for q in range(2)]

        block = ctx.enter_context(nc.Block())

        @block.sync
        def _(sp):
            def load_x(b):
                for h in range(2):
                    js = slice(h * J // 2, (h + 1) * J // 2)
                    sp.dma_start(xs[b % 2][:, js, :], xb[b, :, js, :]).then_inc(x_loaded[b % 2][h], 16)

            load_x(0)
            sp.dma_start(wg[:], Wg.rearrange("(k p) e -> p k e", p=P)).then_inc(router_w_loaded, 16)
            sp.dma_start(bgb[:], bg.rearrange("(a e) -> a e", a=1).to_broadcast([P, E])).then_inc(router_w_loaded, 16)
            sp.dma_start(wqkv[:, :, 0:C], qkv_w.rearrange("(k p) c -> p k c", p=P)).then_inc(attn_w_loaded, 16)
            sp.dma_start(nw[:], norm_w.rearrange("(a c) -> a c", a=1).to_broadcast([P, C])).then_inc(attn_w_loaded, 16)
            sp.dma_start(nb_[:], norm_b.rearrange("(a c) -> a c", a=1).to_broadcast([P, C])).then_inc(attn_w_loaded, 16)
            with nc.allow_non_contiguous_dma(reason="768 bias values, one by one on their partitions"):
                sp.dma_start(qkvb[:], qkv_b.rearrange("(k p) -> p k", p=P)).then_inc(attn_w_loaded, 16)
            sp.dma_start(wp[:], proj_w.rearrange("(k p) c -> p k c", p=P)).then_inc(attn_w_loaded, 16)
            sp.dma_start(bp[:], proj_b.rearrange("(a c) -> a c", a=1).to_broadcast([P, C])).then_inc(attn_w_loaded, 16)
            sp.dma_start(b1rows[:], b1.rearrange("e (k p) -> (e k) p", p=P)).then_inc(b1_loaded, 16)
            load_x(1)
            sp.wait_ge(consts_made, 1)
            sp.dma_start(table.rearrange("(p r) m -> p (r m)", p=P), zeros[:]).then_inc(table_zeroed, 16)

            def load_expert(e, q):
                sp.dma_start(w1[q][:], W1[bass.ds(e, 1)].rearrange("a (k p) h -> p (a k) h", p=P)).then_inc(w_loaded[q], 16)
                sp.dma_start(w2[q][:], W2[bass.ds(e, 1)].rearrange("a (k p) c -> p (a k) c", p=P)).then_inc(w_loaded[q], 16)
                sp.dma_start(b2b[q][:], b2[bass.ds(e, 1)].to_broadcast([P, C])).then_inc(w_loaded[q], 16)

            for q in range(2):
                load_expert(q, q)
            for b in range(NB):
                for h in range(2):
                    sp.wait_ge(o_summed, PAIRS * b + PAIRS // 2 * (h + 1))
                    js = slice(h * J // 2, (h + 1) * J // 2)
                    sp.dma_start(ob[b, :, js, :], osb[b % 2][:, js, :]).then_inc(o_stored[b % 2], 16)
                if b + 2 < NB:
                    sp.wait_ge(o_stored[b % 2], 32 * (b // 2 + 1))
                    sp.wait_ge(meta_scattered[b % 2], 16 * J * (b // 2 + 1))
                    load_x(b + 2)
            for q in range(2):
                sp.wait_ge(meta_scattered[q], NB // 2 * J * 16)
            for _ in range(1):
                sp.dma_start(rec[:].rearrange("p (e m) -> p e m", e=E),
                             table.rearrange("(e p s) m -> p e (s m)", e=E, s=S)).then_inc(rec_loaded, 16)
            with sp.Fori(1, E // 2) as i:
                for q in range(2):
                    sp.wait_ge(y_done, 4 * i - 2 + 2 * q)
                    sp.wait_ge(res_ready, 2 * i - 1 + q)
                    load_expert(2 * i + q, q)
            for q in range(2):
                sp.wait_ge(res_stored[q], E // 2 * S * 16)

        @block.gpsimd
        def _(pool):
            nc.gpsimd.memset(zeros[:], 0.0).then_inc(consts_made, 1)
            nc.gpsimd.memset(ones[:], 1.0).then_inc(consts_made, 1)
            nc.gpsimd.memset(scan_mask[:], 1.0).then_inc(consts_made, 1)
            nc.gpsimd.memset(z[0][:, :, C:ZW], 1.0).then_inc(consts_made, 1)
            nc.gpsimd.memset(z[1][:, :, C:ZW], 1.0).then_inc(consts_made, 1)
            nc.gpsimd.iota(rev[:], pattern=[[-1, E]], base=E, channel_multiplier=0,
                           allow_small_or_imprecise_dtypes=True).then_inc(consts_made, 1)
            nc.gpsimd.iota(token1[:], pattern=[[T, NB], [1, J]], base=1, channel_multiplier=J,
                           allow_small_or_imprecise_dtypes=True).then_inc(consts_made, 1)
            pool.wait_ge(consts_made, 7)
            nc.gpsimd.affine_select(out=ident[:], in_=ones[:], compare_op=ALU.is_equal, fill=0.0, base=0,
                                    pattern=[[-1, P]], channel_multiplier=1).then_inc(consts_made, 1)
            nc.gpsimd.affine_select(out=tri[:], in_=ones[:], compare_op=ALU.is_gt, fill=0.0, base=0,
                                    pattern=[[1, P]], channel_multiplier=-1).then_inc(consts_made, 1)
            nc.gpsimd.memset(scan_mask[:, :, 0:1], 0.0).then_inc(consts_made, 1)
            pool.wait_ge(table_zeroed, 16)
            for b in range(NB):
                pool.wait_ge(meta_ready, b + 1)
                for j in range(J):
                    nc.gpsimd.indirect_dma_start(
                        out=table, out_offset=bass.IndirectOffsetOnAxis(ap=dst[b % 2][:, j:j + 1], axis=0),
                        in_=meta[b % 2][:, j, :], in_offset=None, bounds_check=E * CAP - 1,
                        oob_is_err=False).then_inc(meta_scattered[b % 2], 16)
            pool.wait_ge(o_summed, NB * PAIRS)
            for q in range(2):
                pool.wait_ge(o_stored[q], NB // 2 * 32)
            for q in range(2):
                nc.gpsimd.memset(xg[q][:], 0.0).then_inc(idx_copied, 1)
                nc.gpsimd.memset(res[q][:], 0.0).then_inc(idx_copied, 1)
            pool.wait_ge(ids_ready, 1)
            copied = [4]

            passed = [0]

            def wait_for(semaphore, value, gates=0):
                pool.wait_ge(gate_passed, gates + passed[0])
                pool.wait_ge(semaphore, value)
                nc.gpsimd.tensor_tensor(gate[:], ones[:, 0:2], ones[:, 0:2], ALU.add).then_inc(gate_passed, 1)
                passed[0] += 1

            def take_index(to, e, base, gates):
                copied[0] += 1
                nc.gpsimd.tensor_copy(to[:], ids[:, bass.ds(e * S, S)]).then_inc(idx_copied, 1)
                wait_for(idx_copied, base + copied[0], gates)

            def gather_x(e, q, base=0, gates=0):
                take_index(idx_x[q], e, base, gates)
                for s in range(S):
                    nc.gpsimd.indirect_dma_start(
                        out=xg[q][:, s, :], out_offset=None, in_=xrows,
                        in_offset=bass.IndirectOffsetOnAxis(ap=idx_x[q][:, s:s + 1], axis=0),
                        bounds_check=NTOK - 1, oob_is_err=False).then_inc(xg_loaded[q], 16)

            def gather_res(e, q, base=0, gates=0):
                take_index(idx_o[q], e, base, gates)
                for s in range(S):
                    nc.gpsimd.indirect_dma_start(
                        out=res[q][:, s, :], out_offset=None, in_=orows,
                        in_offset=bass.IndirectOffsetOnAxis(ap=idx_o[q][:, s:s + 1], axis=0),
                        bounds_check=NTOK - 1, oob_is_err=False).then_inc(res_loaded[q], 16)

            def scatter(q):
                for s in range(S):
                    nc.gpsimd.indirect_dma_start(
                        out=orows, out_offset=bass.IndirectOffsetOnAxis(ap=idx_o[q][:, s:s + 1], axis=0),
                        in_=res[q][:, s, :], in_offset=None, bounds_check=NTOK - 1,
                        oob_is_err=False).then_inc(res_stored[q], 16)

            for q in range(2):
                gather_x(q, q)
                gather_res(q, q)
            with pool.Fori(0, E // 2 - 1) as i:
                base, gates = 4 * i, 10 * i
                for q in range(2):
                    e = 2 * i + q
                    wait_for(xn_ready, e + 1, gates)
                    gather_x(e + 2, q, base, gates)
                    wait_for(res_ready, e + 1, gates)
                    scatter(q)
                    wait_for(res_stored[q], S * 16 * (i + 1), gates)
                    gather_res(e + 2, q, base, gates)
            for q in range(2):
                pool.wait_ge(res_ready, E - 1 + q)
                scatter(q)

        @block.tensor
        def _(pe):
            mm = nc.tensor.matmul
            pe.wait_ge(consts_made, 10)
            pe.wait_ge(attn_w_loaded, 96)
            for oc in range(KC):
                for c in range(KC):
                    nc.tensor.transpose(bank[0][:, (oc * KC + c) * P:(oc * KC + c + 1) * P],
                                        wp[:, c, oc * P:(oc + 1) * P], ident[:])
            pe.wait_ge(b1_loaded, 16)
            nc.tensor.transpose(bank[1][:, 0:P], b1rows[:], ident[:]).then_inc(setup_pe, 1)
            pe.wait_ge(setup_dve, 1)
            for kc in range(KC):
                for oc in range(KC):
                    mm(bank[2 + kc][:, 0:C + 1], wqkv[:, KC + oc, kc * P:(kc + 1) * P], wqkv[:, oc, 0:C + 1],
                       start=(oc == 0), stop=(oc == KC - 1))
            for mc in range(KC):
                for oc in range(KC):
                    mm(bank[4][:, mc:mc + 1], wqkv[:, oc, mc * P:(mc + 1) * P], wqkv[:, KC + oc, C:C + 1],
                       start=(oc == 0), stop=(oc == KC - 1))
            for oc in range(KC):
                mm(bank[4][:, KC:KC + 1], wqkv[:, oc, C:C + 1].to_broadcast([P, P]), wqkv[:, KC + oc, C:C + 1],
                   start=(oc == 0), stop=(oc == KC - 1))
            pe.wait_ge(setup_dve, 2)
            for kc in range(KC):
                for oc in range(KC):
                    mm(bank[5][:, kc * C:(kc + 1) * C], wqkv[:, 2 * KC + oc, kc * P:(kc + 1) * P], wpT[:, oc, :],
                       start=(oc == 0), stop=(oc == KC - 1))
            for oc in range(KC):
                last = mm(bank[6][:, 0:C], wqkv[:, 2 * KC + oc, C:C + 1].to_broadcast([P, P]), wpT[:, oc, :],
                          start=(oc == 0), stop=(oc == KC - 1))
            last.then_inc(setup_pe, 1)
            pe.wait_ge(setup_dve, 3)
            pe.wait_ge(router_w_loaded, 32)

            def transposes(q, k):
                for u in range(2):
                    for c in range(KC):
                        last = nc.tensor.transpose(tr_ps[k % 2][:, (c * 2 + u) * P:(c * 2 + u + 1) * P],
                                                   z[q][:, 2 * k + u, c * P:(c + 1) * P], ident[:])
                last.then_inc(tr_done, 1)

            def gram(q, k):
                for u in range(2):
                    j = 2 * k + u
                    for c in range(KC):
                        last = mm(g_ps[c][:, 0:C + 1], z[q][:, j, c * P:(c + 1) * P], z[q][:, j, 0:C + 1],
                                  start=(j == 0), stop=(j == J - 1))
                if k == PAIRS - 1:
                    last.then_inc(g_done, 1)

            def logits(q, k):
                for u in range(2):
                    j = 2 * k + u
                    for c in range(KC):
                        last = mm(lg_ps[q][:, j * E:(j + 1) * E], zT[q][:, c, j * P:(j + 1) * P], wg[:, c, :],
                                  start=(c == 0), stop=(c == KC - 1))
                if k == PAIRS - 1:
                    last.then_inc(logits_done, 1)

            def prefix(q, b):
                pe.wait_ge(count_ready, b + 1)
                mm(lg_ps[q][:, J * E:J * E + E], tri[:], count[:, :, J - 1], start=True, stop=False)
                mm(lg_ps[q][:, J * E:J * E + E], ones[:], total[q][:], start=False, stop=True).then_inc(prefix_done, 1)

            def chain_t(pa, pb, b):
                pe.wait_ge(g_saved, b + 2)
                for c in range(KC):
                    for k in range(KC):
                        mm(pa[:, c * C:(c + 1) * C], G[:, k, c * P:(c + 1) * P], Bm[:, k, :],
                           start=(k == 0), stop=(k == KC - 1))
                for k in range(KC):
                    last = mm(pb[:, 0:C], G[:, k, C:C + 1].to_broadcast([P, P]), Bm[:, k, :],
                              start=(k == 0), stop=(k == KC - 1))
                last.then_inc(chain_done, 1)

            def chain_m(pa, pb, b):
                pe.wait_ge(chain_saved, 2 * b + 1)
                for c in range(KC):
                    for k in range(KC):
                        mm(pa[:, c * C:(c + 1) * C], AT[:, k, c * P:(c + 1) * P], Tm[:, k, :],
                           start=(k == 0), stop=(k == KC - 1))
                for k in range(KC):
                    last = mm(pb[:, 0:C], AT[:, k, C:C + 1].to_broadcast([P, P]), Tm[:, k, :],
                              start=(k == 0), stop=(k == KC - 1))
                last.then_inc(chain_done, 1)

            def out_pair(q, k):
                for u in range(2):
                    j = 2 * k + u
                    for c in range(KC):
                        last = mm(o_ps[k % 2][:, u * C:(u + 1) * C], zT[q][:, c, j * P:(j + 1) * P], M[q][:, c, :],
                                  start=(c == 0), stop=(c == KC - 1))
                last.then_inc(o_done, 1)

            with pe.Fori(0, NB // 2) as i:
                for q in range(2):
                    b = 2 * i + q
                    pe.wait_ge(z_ready, PAIRS * b + 1)
                    transposes(q, 0)
                    for k in range(PAIRS):
                        if k + 1 < PAIRS:
                            pe.wait_ge(z_ready, PAIRS * b + k + 2)
                            transposes(q, k + 1)
                        if k == 0:
                            pe.wait_ge(g_saved, b + 1)
                        gram(q, k)
                        pe.wait_ge(zT_ready, PAIRS * b + k + 1)
                        logits(q, k)
                        if q == 1 and k == 1:
                            chain_t(o_ps[0], o_ps[1], 2 * i)
                        if q == 1 and k == 3:
                            prefix(0, 2 * i)
                        if q == 1 and k == 4:
                            chain_m(o_ps[0], o_ps[1], 2 * i)
                pe.wait_ge(chain_saved, 4 * i + 2)
                for k in range(PAIRS):
                    if k >= 2:
                        pe.wait_ge(o_summed, PAIRS * 2 * i + k - 1)
                    out_pair(0, k)
                    if k == 0:
                        chain_t(tr_ps[0], tr_ps[1], 2 * i + 1)
                    if k == 2:
                        prefix(1, 2 * i + 1)
                    if k == 3:
                        chain_m(tr_ps[0], tr_ps[1], 2 * i + 1)
                pe.wait_ge(chain_saved, 4 * i + 4)
                for k in range(PAIRS):
                    pe.wait_ge(o_summed, PAIRS * (2 * i + 1) + k - 1)
                    out_pair(1, k)

            def xn_transposes(e, q):
                pe.wait_ge(xn_ready, e + 1)
                for c in range(KC):
                    for s in range(S):
                        last = nc.tensor.transpose(xt_ps[c][:, s * P:(s + 1) * P],
                                                   xn[q][:, s, c * P:(c + 1) * P], ident[:])
                    last.then_inc(xt_done, 1)

            def expert(i, q, last_one=False):
                e = 2 * i + q
                pe.wait_ge(w_loaded[q], 48 * i + 48)
                pe.wait_ge(xnT_ready, 2 * e + 2)
                for n in range(HC):
                    if n >= 4:
                        pe.wait_ge(h_act if n % 2 == 0 else h_dve, 4 * e + (n - 4) // 2 + 1)
                    for c in range(KC):
                        last = mm(h_ps[n % 4][:], w1[q][:, c, n * P:(n + 1) * P], xnT[:, c, :],
                                  start=(c == 0), stop=(c == KC - 1))
                    last.then_inc(h_done, 1)
                if not last_one:
                    xn_transposes(e + 1, 1 - q)
                pe.wait_ge(h_act, 4 * e + 4)
                pe.wait_ge(h_dve, 4 * e + 4)
                for s in range(S):
                    if s % 2 == 0:
                        pe.wait_ge(y_free, 2 * e + s // 2 + 1)
                    for n in range(HC):
                        last = mm(y_ps[s // 2][:, s % 2 * C:(s % 2 + 1) * C], hT[:, n, s * P:(s + 1) * P],
                                  w2[q][:, n, :], start=(n == 0), stop=(n == HC - 1))
                    if s % 2 == 1:
                        last.then_inc(y_done, 1)

            pe.wait_ge(o_summed, NB * PAIRS)
            xn_transposes(0, 0)
            with pe.Fori(0, E // 2 - 1) as i:
                expert(i, 0)
                expert(i, 1)
            expert(E // 2 - 1, 0)
            expert(E // 2 - 1, 1, last_one=True)

        @block.scalar
        def _(act):
            def roots(q, b):
                act.wait_ge(var_ready, b + 1)
                nc.scalar.activation(stds[q][:], var2[q][:], ACT.Sqrt).then_inc(std_ready, 1)

            def save_zT(q, b, k):
                act.wait_ge(tr_done, PAIRS * b + k + 1)
                nc.scalar.activation(zT[q][:, :, 2 * k * P:(2 * k + 2) * P],
                                     tr_ps[k % 2][:].rearrange("p (c t) -> p c t", c=KC), ACT.Copy).then_inc(zT_ready, 1)

            def exps(b):
                act.wait_ge(shifted_ready, b + 1)
                nc.scalar.activation(Ex[:], D[:], ACT.Exp).then_inc(exp_ready, 1)

            with act.Fori(0, NB // 2) as i:
                roots(0, 2 * i)
                for k in range(PAIRS):
                    if k == 3:
                        roots(1, 2 * i + 1)
                    save_zT(0, 2 * i, k)
                for k in range(PAIRS):
                    save_zT(1, 2 * i + 1, k)
                    if k == 2:
                        exps(2 * i)
                exps(2 * i + 1)

            def save_xnT(e):
                act.wait_ge(xt_done, 2 * e + 1)
                nc.scalar.activation(xnT[:, 0, :], xt_ps[0][:], ACT.Copy).then_inc(xnT_ready, 1)
                act.wait_ge(xt_done, 2 * e + 2)
                nc.scalar.activation(xnT[:, 1, :], xt_ps[1][:], ACT.Copy).then_inc(xnT_ready, 1)

            def hidden(e):
                for n in range(0, HC, 2):
                    act.wait_ge(h_done, HC * e + n + 1)
                    nc.scalar.activation(hT[:, n, :], h_ps[n % 4][:], ACT.Relu,
                                         bias=b1T[:, bass.ds(e * HC + n, 1)]).then_inc(h_act, 1)

            save_xnT(0)
            with act.Fori(0, E // 2 - 1) as i:
                for q in range(2):
                    hidden(2 * i + q)
                    save_xnT(2 * i + q + 1)
            hidden(E - 2)
            save_xnT(E - 1)
            hidden(E - 1)

        @block.vector
        def _(dve):
            v = nc.vector
            at = [0]
            start = [0]

            def link(op):
                op.then_inc(dve_chain, 1)
                at[0] += 1
                dve.wait_ge(dve_chain, start[0] + at[0])

            dve.wait_ge(attn_w_loaded, 96)
            for o in range(6):
                link(v.tensor_tensor_reduce(L[:].rearrange("p j e -> p (j e)"), wqkv[:, o, 0:C], nb_[:], 1.0, 0.0,
                                            ALU.mult, ALU.add, dots[:, o:o + 1]))
            v.tensor_tensor(wqkv[:, :, 0:C], wqkv[:, :, 0:C], nw[:].rearrange("p (a c) -> p a c", a=1).to_broadcast([P, 6, C]),
                            ALU.mult)
            link(v.memset(wqkv[:, :, C:ZW], 0.0))
            v.memset(total[0][:], 0.0)
            v.tensor_tensor(wqkv[:, :, C], dots[:], qkvb[:], ALU.add).then_inc(setup_dve, 1)
            dve.wait_ge(setup_pe, 1)
            link(v.tensor_copy(wpT[:].rearrange("p a c -> p (a c)"), bank[0][:]))
            v.tensor_copy(b1T[:], bank[1][:, 0:P]).then_inc(setup_dve, 1)
            dve.wait_ge(setup_pe, 2)
            scale = float(C) ** -0.5
            for kc in range(KC):
                v.tensor_scalar(AT[:, kc, :], bank[2 + kc][:, 0:C + 1], scale, None, ALU.mult)
            v.tensor_scalar(Acol[:], bank[4][:, 0:KC], scale, None, ALU.mult)
            v.tensor_scalar(Alast[:], bank[4][:, KC:KC + 1], scale, None, ALU.mult)
            v.tensor_scalar(Bsum[:], bank[6][:, 0:C], float(T), None, ALU.mult)
            v.tensor_copy(Blast[:], bank[6][:, 0:C])
            link(v.tensor_copy(Bm[:].rearrange("p k c -> p (k c)"), bank[5][:]))
            dve.wait_ge(consts_made, 10)
            dve.wait_ge(router_w_loaded, 32)
            v.memset(s1[:, 7, :], 0.0).then_inc(setup_dve, 1)
            v.memset(s1[:, 6, :], 0.0).then_inc(g_saved, 1)

            def stats(i, q):
                for j in range(J):
                    if j % (J // 2) == 0:
                        dve.wait_ge(x_loaded[q][j // (J // 2)], 16 * i + 16)
                    last = v.bn_stats(st[:, j, :], xs[q][:, j, :])
                link(last)
                me, mo, ve, vo = st[:, :, 1], st[:, :, 4], st[:, :, 2], st[:, :, 5]
                v.tensor_tensor(s1[:, 0, :], me, mo, ALU.add)
                v.tensor_tensor(s1[:, 1, :], me, mo, ALU.subtract)
                link(v.tensor_tensor(s1[:, 2, :], ve, vo, ALU.add))
                v.tensor_scalar(mean[q][:], s1[:, 0, :], 0.5, None, ALU.mult)
                v.tensor_tensor(s1[:, 3, :], s1[:, 1, :], s1[:, 1, :], ALU.mult)
                link(v.tensor_scalar(s1[:, 4, :], s1[:, 2, :], 1.0 / C, None, ALU.mult))
                link(v.scalar_tensor_tensor(s1[:, 5, :], s1[:, 3, :], 0.25, s1[:, 4, :], ALU.mult, ALU.add))
                link(v.tensor_scalar(var2[q][:, 0, :], s1[:, 5, :], EPS, None, ALU.add))
                v.scalar_tensor_tensor(var2[q][:, 1, :], var2[q][:, 0, :], EPS, s1[:, 5, :],
                                       ALU.mult, ALU.add).then_inc(var_ready, 1)

            def normalise(b, q):
                dve.wait_ge(std_ready, b + 1)
                link(v.reciprocal(rstd[q][:], stds[q][:]))
                for k in range(PAIRS):
                    for j in (2 * k, 2 * k + 1):
                        last = v.tensor_scalar(z[q][:, j, 0:C], xs[q][:, j, :], mean[q][:, j:j + 1],
                                               rstd[q][:, 1, j:j + 1], ALU.subtract, ALU.mult)
                    last.then_inc(z_ready, 1)
                v.tensor_tensor(s2[q][:], stds[q][:, 1, :], rstd[q][:, 0, :], ALU.mult)
                v.tensor_scalar(rp1[q][:], rstd[q][:, 0, :], 1.0, None, ALU.add)
                link(v.scalar_tensor_tensor(nmr[q][:], mean[q][:], -1.0, rstd[q][:, 0, :], ALU.mult, ALU.mult))

            def over_e(ap):
                return ap.rearrange("p (j a) -> p j a", a=1).to_broadcast([P, J, E])

            def over_j(ap):
                return ap.rearrange("p (a e) -> p a e", a=1).to_broadcast([P, J, E])

            def route_1(b, q):
                dve.wait_ge(logits_done, b + 1)
                link(v.tensor_tensor(key[:], lg_ps[q][:, 0:J * E].rearrange("p (j e) -> p j e", e=E), over_e(s2[q][:]), ALU.mult))
                link(v.tensor_tensor(L[:], key[:], over_j(bgb[:]), ALU.add))
                link(v.tensor_reduce(r1[:, 0, :], L[:], AX, ALU.max))
                v.tensor_tensor(D[:], L[:], over_e(r1[:, 0, :]), ALU.subtract).then_inc(shifted_ready, 1)
                dve.wait_ge(shifted_ready, b + 1)
                link(v.scalar_tensor_tensor(key[:], D[:], 0.0, over_j(rev[:]), ALU.is_ge, ALU.mult))
                link(v.tensor_reduce(r1[:, 1, :], key[:], AX, ALU.max))
                link(v.tensor_tensor(onehot[:].rearrange("p e j -> p j e"), over_j(rev[:]), over_e(r1[:, 1, :]), ALU.is_equal))
                v.tensor_tensor_scan(count[:].rearrange("p e j -> p (e j)"), scan_mask[:].rearrange("p e j -> p (e j)"),
                                     onehot[:].rearrange("p e j -> p (e j)"), 0.0, ALU.mult, ALU.add).then_inc(count_ready, 1)
                dve.wait_ge(count_ready, b + 1)
                v.tensor_scalar(r1[:, 2, :], r1[:, 1, :], -float(CAP), float(E * CAP - 1), ALU.mult, ALU.add)
                link(v.tensor_tensor(total[1 - q][:], total[q][:], count[:, :, J - 1], ALU.add))

            def route_2(b, q):
                dve.wait_ge(prefix_done, b + 1)
                link(v.tensor_tensor(posm[:], count[:], lg_ps[q][:, J * E:J * E + E].rearrange("p (e a) -> p e a", a=1).to_broadcast([P, E, J]), ALU.add))
                link(v.tensor_tensor(key[:].rearrange("p j e -> p e j"), posm[:], onehot[:], ALU.mult))
                link(v.tensor_reduce(r1[:, 3, :], key[:], AX, ALU.add))
                v.tensor_tensor(r1[:, 4, :], r1[:, 3, :], r1[:, 2, :], ALU.add)
                link(v.tensor_scalar(r1[:, 5, :], r1[:, 3, :], float(CAP), SKIP, ALU.is_gt, ALU.mult))
                v.tensor_tensor(dst[q][:], r1[:, 4, :], r1[:, 5, :], ALU.add)
                v.tensor_copy(meta[q][:, :, 0], token1[:, bass.ds(b * J, J)])
                v.tensor_copy(meta[q][:, :, 1], mean[q][:])
                v.tensor_copy(meta[q][:, :, 2], rstd[q][:, 0, :])
                dve.wait_ge(exp_ready, b + 1)
                link(v.tensor_reduce(r1[:, 6, :], Ex[:], AX, ALU.add))
                v.reciprocal(meta[q][:, :, 3], r1[:, 6, :]).then_inc(meta_ready, 1)

            def save_gram(b):
                dve.wait_ge(g_done, b + 1)
                v.tensor_copy(G[:, 0, :], g_ps[0][:, 0:C + 1])
                v.tensor_copy(G[:, 1, :], g_ps[1][:, 0:C + 1]).then_inc(g_saved, 1)
                dve.wait_ge(g_saved, b + 2)

            def save_t(pa, pb, b):
                dve.wait_ge(chain_done, 2 * b + 1)
                v.scalar_tensor_tensor(Tlast[:], pb[:, 0:C], 1.0, Bsum[:], ALU.mult, ALU.add)
                for c in range(KC):
                    last = v.scalar_tensor_tensor(Tm[:, c, :], Blast[:], G[:, c, C:C + 1], pa[:, c * C:(c + 1) * C],
                                                  ALU.mult, ALU.add)
                last.then_inc(chain_saved, 1)
                dve.wait_ge(chain_saved, 2 * b + 1)

            def save_m(pa, pb, b, q):
                dve.wait_ge(chain_done, 2 * b + 2)
                for c in range(KC):
                    v.scalar_tensor_tensor(M[q][:, c, :], Tlast[:], Acol[:, c:c + 1], pa[:, c * C:(c + 1) * C],
                                           ALU.mult, ALU.add)
                link(v.scalar_tensor_tensor(cb[q][:], Tlast[:], Alast[:, 0:1], pb[:, 0:C], ALU.mult, ALU.add))
                v.tensor_tensor(cb[q][:], cb[q][:], bp[:], ALU.add).then_inc(chain_saved, 1)
                dve.wait_ge(chain_saved, 2 * b + 2)

            def sum_pair(i, b, q, k):
                for u in range(2):
                    j = 2 * k + u
                    last = v.scalar_tensor_tensor(osb[q][:, j, :], xs[q][:, j, :], rp1[q][:, j:j + 1], cb[q][:],
                                                  ALU.mult, ALU.add)
                link(last)
                dve.wait_ge(o_done, PAIRS * b + k + 1)
                for u in range(2):
                    j = 2 * k + u
                    last = v.scalar_tensor_tensor(osb[q][:, j, :], o_ps[k % 2][:, u * C:(u + 1) * C], nmr[q][:, j:j + 1],
                                                  osb[q][:, j, :], ALU.add, ALU.add)
                last.then_inc(o_summed, 1)

            BODY = 56
            before = at[0]
            at[0] = 0
            with dve.Fori(0, NB // 2) as i:
                start[0] = i * BODY + before
                stats(i, 0)
                normalise(2 * i, 0)
                stats(i, 1)
                normalise(2 * i + 1, 1)
                save_gram(2 * i)
                route_1(2 * i, 0)
                save_t(o_ps[0], o_ps[1], 2 * i)
                route_2(2 * i, 0)
                save_m(o_ps[0], o_ps[1], 2 * i, 0)
                save_gram(2 * i + 1)
                sum_pair(i, 2 * i, 0, 0)
                route_1(2 * i + 1, 1)
                save_t(tr_ps[0], tr_ps[1], 2 * i + 1)
                for k in (1, 2):
                    sum_pair(i, 2 * i, 0, k)
                route_2(2 * i + 1, 1)
                sum_pair(i, 2 * i, 0, 3)
                save_m(tr_ps[0], tr_ps[1], 2 * i + 1, 1)
                for k in range(4, PAIRS):
                    sum_pair(i, 2 * i, 0, k)
                for k in range(PAIRS):
                    sum_pair(i, 2 * i + 1, 1, k)
            assert at[0] == BODY, at[0]
            start[0] = before + (NB // 2) * BODY
            at[0] = 0

            dve.wait_ge(rec_loaded, 16)
            slots = rec[:].rearrange("p (n m) -> p n m", m=META)
            v.tensor_scalar(idf[:, 0, :], slots[:, :, 0], 0.0, SKIP, ALU.is_equal, ALU.mult)
            link(v.tensor_scalar(idf[:, 1, :], slots[:, :, 0], 1.0, None, ALU.subtract))
            v.tensor_tensor(ids[:], idf[:, 0, :], idf[:, 1, :], ALU.add).then_inc(ids_ready, 1)
            v.memset(s1[:, 6, :], 0.0).then_inc(y_free, 2)

            def record(e, s, m):
                return rec[:, bass.ds((e * S + s) * META + m, 1)]

            def normalise_rows(i, q, e):
                dve.wait_ge(xg_loaded[q], 16 * S * (i + 1))
                for s in range(S):
                    last = v.tensor_scalar(xn[q][:, s, :], xg[q][:, s, :], record(e, s, 1), record(e, s, 2),
                                           ALU.subtract, ALU.mult)
                last.then_inc(xn_ready, 1)

            def hidden(e, n):
                dve.wait_ge(h_done, HC * e + n + 1)
                v.tensor_scalar(hT[:, n, :], h_ps[n % 4][:], b1T[:, bass.ds(e * HC + n, 1)], 0.0,
                                ALU.add, ALU.max).then_inc(h_dve, 1)

            def expert(i, q, last_one=False):
                e = 2 * i + q
                hidden(e, 1)
                hidden(e, 3)
                if not last_one:
                    normalise_rows(i + q, 1 - q, e + 1)
                hidden(e, 5)
                hidden(e, 7)
                dve.wait_ge(res_loaded[q], 16 * S * (i + 1))
                dve.wait_ge(w_loaded[q], 48 * (i + 1))
                for s in range(S):
                    last = v.scalar_tensor_tensor(res[q][:, s, :], b2b[q][:], record(e, s, 3), res[q][:, s, :],
                                                  ALU.mult, ALU.add)
                link(last)
                for s in range(S):
                    if s % 2 == 0:
                        dve.wait_ge(y_done, 2 * e + s // 2 + 1)
                    last = v.scalar_tensor_tensor(res[q][:, s, :], y_ps[s // 2][:, s % 2 * C:(s % 2 + 1) * C],
                                                  record(e, s, 3), res[q][:, s, :], ALU.mult, ALU.add)
                    if s == 1:
                        last.then_inc(y_free, 1)
                last.then_inc(y_free, 1)
                dve.wait_ge(y_free, 2 * e + 4)
                v.memset(s1[:, 6, :], 0.0).then_inc(res_ready, 1)

            normalise_rows(0, 0, 0)
            base = start[0] + at[0]
            at[0] = 0
            with dve.Fori(0, E // 2 - 1) as i:
                start[0] = base + 2 * i
                expert(i, 0)
                expert(i, 1)
            assert at[0] == 2
            start[0] = base + 2 * (E // 2 - 1)
            at[0] = 0
            expert(E // 2 - 1, 0)
            expert(E // 2 - 1, 1, last_one=True)


_INS = ["L0_attn_x", "L0_attn_norm_w", "L0_attn_norm_b", "L0_attn_qkv_w", "L0_attn_qkv_b", "L0_attn_proj_w",
        "L0_attn_proj_b", "L0_ffn_Wg", "L0_ffn_bg", "L0_ffn_W1", "L0_ffn_b1", "L0_ffn_W2", "L0_ffn_b2"]


def kernel(**inputs):
    import numpy as np
    import concourse.bacc as bacc
    from concourse.bass_utils import run_bass_kernel_spmd

    nc = bacc.Bacc("TRN2", target_bir_lowering=False, num_devices=1)
    arrays, args = {}, []
    for name in _INS:
        a = np.ascontiguousarray(inputs[name])
        arrays[f"in_{name}"] = a
        args.append(nc.dram_tensor(f"in_{name}", a.shape, mybir.dt.from_np(a.dtype), kind="ExternalInput").ap())
    out = nc.dram_tensor("out", (NB, T, C), F32, kind="ExternalOutput").ap()
    program(nc, *args, out)
    r = run_bass_kernel_spmd(nc, [arrays], core_ids=[0])
    return r.results[0]["out"]
```

```python
from contextlib import ExitStack

import concourse.bass as bass
from concourse import mybir
from concourse.alu_op_type import AluOpType as ALU

ACT = mybir.ActivationFunctionType
F32 = mybir.dt.float32
F32R = mybir.dt.float32r
U32 = mybir.dt.uint32
AX = mybir.AxisListType.X

P = 128
NB = 4
T = 2048
C = 256
KC = C // P
J = T // P
PAIRS = J // 2
E = 16
H = 1024
HC = H // P
NTOK = NB * T
CAP = -(-NTOK // E)
S = CAP // P
EPS = 1e-5
ZW = C + 2
SKIP = 2.0 * NTOK
PIECES = 4
META = 4


def program(nc, x, norm_w, norm_b, qkv_w, qkv_b, proj_w, proj_b, Wg, bg, W1, b1, W2, b2, out):
    table = nc.dram_tensor("slot_records", (E * CAP, META), F32).ap()
    xrows = x.rearrange("b t c -> (b t) c")
    orows = out.rearrange("b t c -> (b t) c")
    xb = x.rearrange("b (p j) c -> b p j c", j=J)
    ob = out.rearrange("b (p j) c -> b p j c", j=J)

    with ExitStack() as ctx:
        def sb(name, shape, dt=F32, stack=None):
            return (stack or ctx).enter_context(nc.sbuf_tensor(name, shape, dt))

        def sem(name):
            return ctx.enter_context(nc.semaphore(name))

        def two(name, shape, dt=F32, stack=None):
            return [sb(f"{name}{q}", shape, dt, stack) for q in range(2)]

        bank = [ctx.enter_context(nc.psum_tensor(f"bank{n}", [P, 512], F32)) for n in range(8)]
        tr_ps, g_ps, lg_ps, o_ps = bank[0:2], bank[2:4], bank[4:6], bank[6:8]
        h_ps, y_ps, xt_ps = bank[0:4], bank[4:6], bank[6:8]

        ident = sb("ident", [P, P])
        tri = sb("tri", [P, P])
        ones = sb("ones", [P, P])
        zeros = sb("zeros", [P, E * CAP * META // P])
        scan_mask = sb("scan_mask", [P, E, J])
        rev = sb("rev", [P, E])
        token1 = sb("token1", [P, NB * J])
        wqkv = sb("wqkv", [P, 6, ZW])
        wp = sb("wp", [P, KC, C])
        wpT = sb("wpT", [P, KC, C])
        nw = sb("nw", [P, C])
        nb_ = sb("nb", [P, C])
        dots = sb("dots", [P, 6])
        qkvb = sb("qkvb", [P, 6])
        bp = sb("bp", [P, C])
        AT = sb("AT", [P, KC, C + 1])
        Acol = sb("Acol", [P, KC])
        Alast = sb("Alast", [P, 1])
        Bm = sb("Bm", [P, KC, C])
        Blast = sb("Blast", [P, C])
        Bsum = sb("Bsum", [P, C])
        wg = sb("wg", [P, KC, E])
        bgb = sb("bgb", [P, E])
        b1rows = sb("b1rows", [P, P])
        b1T = sb("b1T", [P, E * HC])
        G = sb("G", [P, KC, C + 1])
        Tm = sb("Tm", [P, KC, C])
        Tlast = sb("Tlast", [P, C])
        M = two("M", [P, KC, C])
        cb = two("cb", [P, C])
        st = sb("st", [P, J, 6])
        s1 = sb("s1", [P, 8, J])
        stds = two("stds", [P, 2, J])
        var2 = two("var2", [P, 2, J])
        mean = two("mean", [P, J])
        rstd = two("rstd", [P, 2, J])
        s2 = two("s2", [P, J])
        rp1 = two("rp1", [P, J])
        nmr = two("nmr", [P, J])
        L = sb("L", [P, J, E])
        D = sb("D", [P, J, E])
        Ex = sb("Ex", [P, J, E])
        key = sb("key", [P, J, E])
        onehot = sb("onehot", [P, E, J])
        count = sb("count", [P, E, J])
        posm = sb("posm", [P, E, J])
        r1 = sb("r1", [P, 8, J])
        total = two("total", [P, E])
        dst = two("dst", [P, J], U32)
        meta = two("meta", [P, J, META])
        w1 = sb("w1", [P, KC, H])
        w2 = sb("w2", [P, HC, C])
        b2b = two("b2b", [P, C])
        rec = sb("rec", [P, E * S * META])
        idf = sb("idf", [P, 3, E * S])
        ids = sb("ids", [P, E * S], U32)
        idx_x = two("idx_x", [P, S], U32)
        idx_o = two("idx_o", [P, S], U32)
        gate = sb("gate", [P, 2])
        xg = two("xg", [P, S, C])
        w1_hi = [sb("w1_hi0", [P, KC, H], F32R)]
        w1_lo = [sb("w1_lo0", [P, KC, H], F32R)]
        w2_hi = [sb("w2_hi0", [P, HC, C], F32R)]
        w2_lo = [sb("w2_lo0", [P, HC, C], F32R)]

        early = ctx.enter_context(ExitStack())
        xs = two("xs", [P, J, C], stack=early)
        z = two("z", [P, J, ZW], stack=early)
        zT = two("zT", [P, KC, T], stack=early)
        osb = [t[:, :, 0:C] for t in z]
        early.close()
        xn = two("xn", [P, S, C])
        xnT_hi = sb("xnT_hi", [P, KC, CAP], F32R)
        xnT_lo = sb("xnT_lo", [P, KC, CAP], F32R)
        hT_hi = sb("hT_hi", [P, HC, CAP], F32R)
        w1_hi.append(sb("w1_hi1", [P, KC, H], F32R))
        w1_lo.append(sb("w1_lo1", [P, KC, H], F32R))
        w2_hi.append(sb("w2_hi1", [P, HC, C], F32R))
        w2_lo.append(sb("w2_lo1", [P, HC, C], F32R))
        res = two("res", [P, S, C])
        relu = two("relu", [P, CAP])
        hT_lo = sb("hT_lo", [P, HC, CAP], F32R)

        consts_made = sem("consts_made")
        attn_w_loaded = sem("attn_w_loaded")
        router_w_loaded = sem("router_w_loaded")
        x_loaded = [[sem(f"x_loaded{q}{h}") for h in range(2)] for q in range(2)]
        table_zeroed = sem("table_zeroed")
        w1_loaded = sem("w1_loaded")
        w2_loaded = sem("w2_loaded")
        b2_loaded = [sem(f"b2_loaded{q}") for q in range(2)]
        w_hi_ready = sem("w_hi_ready")
        w_lo_ready = sem("w_lo_ready")
        b1_loaded = sem("b1_loaded")
        setup_pe = sem("setup_pe")
        setup_dve = sem("setup_dve")
        dve_chain = sem("dve_chain")
        var_ready = sem("var_ready")
        std_ready = sem("std_ready")
        z_ready = sem("z_ready")
        tr_done = sem("tr_done")
        zT_ready = sem("zT_ready")
        g_done = sem("g_done")
        g_saved = sem("g_saved")
        logits_done = sem("logits_done")
        shifted_ready = sem("shifted_ready")
        exp_ready = sem("exp_ready")
        count_ready = sem("count_ready")
        prefix_done = sem("prefix_done")
        chain_done = sem("chain_done")
        chain_saved = sem("chain_saved")
        meta_ready = sem("meta_ready")
        meta_scattered = [sem(f"meta_scattered{q}") for q in range(2)]
        o_done = sem("o_done")
        o_summed = sem("o_summed")
        o_stored = [sem(f"o_stored{q}") for q in range(2)]
        rec_loaded = sem("rec_loaded")
        ids_ready = sem("ids_ready")
        idx_copied = sem("idx_copied")
        gate_passed = sem("gate_passed")
        xg_loaded = [sem(f"xg_loaded{q}") for q in range(2)]
        res_loaded = [sem(f"res_loaded{q}") for q in range(2)]
        xn_ready = sem("xn_ready")
        xt_done = sem("xt_done")
        xnT_hi_ready = sem("xnT_hi_ready")
        xnT_lo_ready = sem("xnT_lo_ready")
        h_done = sem("h_done")
        h_hi_ready = sem("h_hi_ready")
        h_lo_ready = sem("h_lo_ready")
        y_done = sem("y_done")
        y_free = sem("y_free")
        res_ready = sem("res_ready")
        res_stored = [sem(f"res_stored{q}") for q in range(2)]

        def weight_piece(q, n):
            if n < 2:
                return w1[:, n, :], w1_hi[q][:, n, :], w1_lo[q][:, n, :]
            ks = slice((n - 2) * HC // 2, (n - 1) * HC // 2)
            return w2[:, ks, :], w2_hi[q][:, ks, :], w2_lo[q][:, ks, :]

        block = ctx.enter_context(nc.Block())

        @block.sync
        def _(sp):
            def load_x(b):
                for h in range(2):
                    js = slice(h * J // 2, (h + 1) * J // 2)
                    sp.dma_start(xs[b % 2][:, js, :], xb[b, :, js, :]).then_inc(x_loaded[b % 2][h], 16)

            load_x(0)
            sp.dma_start(wg[:], Wg.rearrange("(k p) e -> p k e", p=P)).then_inc(router_w_loaded, 16)
            sp.dma_start(bgb[:], bg.rearrange("(a e) -> a e", a=1).to_broadcast([P, E])).then_inc(router_w_loaded, 16)
            sp.dma_start(wqkv[:, :, 0:C], qkv_w.rearrange("(k p) c -> p k c", p=P)).then_inc(attn_w_loaded, 16)
            sp.dma_start(nw[:], norm_w.rearrange("(a c) -> a c", a=1).to_broadcast([P, C])).then_inc(attn_w_loaded, 16)
            sp.dma_start(nb_[:], norm_b.rearrange("(a c) -> a c", a=1).to_broadcast([P, C])).then_inc(attn_w_loaded, 16)
            with nc.allow_non_contiguous_dma(reason="768 bias values, one by one on their partitions"):
                sp.dma_start(qkvb[:], qkv_b.rearrange("(k p) -> p k", p=P)).then_inc(attn_w_loaded, 16)
            sp.dma_start(wp[:], proj_w.rearrange("(k p) c -> p k c", p=P)).then_inc(attn_w_loaded, 16)
            sp.dma_start(bp[:], proj_b.rearrange("(a c) -> a c", a=1).to_broadcast([P, C])).then_inc(attn_w_loaded, 16)
            sp.dma_start(b1rows[:], b1.rearrange("e (k p) -> (e k) p", p=P)).then_inc(b1_loaded, 16)
            load_x(1)
            sp.wait_ge(consts_made, 1)
            sp.dma_start(table.rearrange("(p r) m -> p (r m)", p=P), zeros[:]).then_inc(table_zeroed, 16)

            def load_weights(e):
                sp.dma_start(w1[:], W1[bass.ds(e, 1)].rearrange("a (k p) h -> p (a k) h", p=P)).then_inc(w1_loaded, 16)
                sp.dma_start(w2[:], W2[bass.ds(e, 1)].rearrange("a (k p) c -> p (a k) c", p=P)).then_inc(w2_loaded, 16)

            def load_bias(e, q):
                sp.dma_start(b2b[q][:], b2[bass.ds(e, 1)].to_broadcast([P, C])).then_inc(b2_loaded[q], 16)

            load_weights(0)
            load_bias(0, 0)
            load_bias(1, 1)
            for b in range(NB):
                for h in range(2):
                    sp.wait_ge(o_summed, PAIRS * b + PAIRS // 2 * (h + 1))
                    js = slice(h * J // 2, (h + 1) * J // 2)
                    sp.dma_start(ob[b, :, js, :], osb[b % 2][:, js, :]).then_inc(o_stored[b % 2], 16)
                if b + 2 < NB:
                    sp.wait_ge(o_stored[b % 2], 32 * (b // 2 + 1))
                    sp.wait_ge(meta_scattered[b % 2], 16 * J * (b // 2 + 1))
                    load_x(b + 2)
            sp.wait_ge(w_lo_ready, PIECES)
            load_weights(1)
            with sp.Fori(1, E // 2) as i:
                for q in range(2):
                    sp.wait_ge(w_lo_ready, PIECES * 2 * i + PIECES * q)
                    load_weights(2 * i + q)
                    sp.wait_ge(res_ready, 2 * i - 1 + q)
                    load_bias(2 * i + q, q)
            for q in range(2):
                sp.wait_ge(res_stored[q], E // 2 * S * 16)

        @block.gpsimd
        def _(pool):
            nc.gpsimd.memset(zeros[:], 0.0).then_inc(consts_made, 1)
            nc.gpsimd.memset(ones[:], 1.0).then_inc(consts_made, 1)
            nc.gpsimd.memset(scan_mask[:], 1.0).then_inc(consts_made, 1)
            nc.gpsimd.memset(z[0][:, :, C:ZW], 1.0).then_inc(consts_made, 1)
            nc.gpsimd.memset(z[1][:, :, C:ZW], 1.0).then_inc(consts_made, 1)
            nc.gpsimd.iota(rev[:], pattern=[[-1, E]], base=E, channel_multiplier=0,
                           allow_small_or_imprecise_dtypes=True).then_inc(consts_made, 1)
            nc.gpsimd.iota(token1[:], pattern=[[T, NB], [1, J]], base=1, channel_multiplier=J,
                           allow_small_or_imprecise_dtypes=True).then_inc(consts_made, 1)
            pool.wait_ge(consts_made, 7)
            nc.gpsimd.affine_select(out=ident[:], in_=ones[:], compare_op=ALU.is_equal, fill=0.0, base=0,
                                    pattern=[[-1, P]], channel_multiplier=1).then_inc(consts_made, 1)
            nc.gpsimd.affine_select(out=tri[:], in_=ones[:], compare_op=ALU.is_gt, fill=0.0, base=0,
                                    pattern=[[1, P]], channel_multiplier=-1).then_inc(consts_made, 1)
            nc.gpsimd.memset(scan_mask[:, :, 0:1], 0.0).then_inc(consts_made, 1)
            pool.wait_ge(table_zeroed, 16)
            for b in range(NB):
                pool.wait_ge(meta_ready, b + 1)
                for j in range(J):
                    nc.gpsimd.indirect_dma_start(
                        out=table, out_offset=bass.IndirectOffsetOnAxis(ap=dst[b % 2][:, j:j + 1], axis=0),
                        in_=meta[b % 2][:, j, :], in_offset=None, bounds_check=E * CAP - 1,
                        oob_is_err=False).then_inc(meta_scattered[b % 2], 16)
            for q in range(2):
                nc.gpsimd.memset(xg[q][:], 0.0).then_inc(idx_copied, 1)
            pool.wait_ge(rec_loaded, 16)
            slots = rec[:].rearrange("p (n m) -> p n m", m=META)
            nc.gpsimd.tensor_scalar(idf[:, 0, :], slots[:, :, 0], 0.0, SKIP, ALU.is_equal, ALU.mult).then_inc(ids_ready, 1)
            nc.gpsimd.tensor_scalar(idf[:, 1, :], slots[:, :, 0], 1.0, None, ALU.subtract).then_inc(ids_ready, 1)
            pool.wait_ge(ids_ready, 2)
            nc.gpsimd.tensor_tensor(idf[:, 2, :], idf[:, 0, :], idf[:, 1, :], ALU.add).then_inc(ids_ready, 1)
            pool.wait_ge(ids_ready, 3)
            nc.gpsimd.tensor_copy(ids[:], idf[:, 2, :]).then_inc(ids_ready, 1)
            pool.wait_ge(ids_ready, 4)
            copied = [2]

            passed = [0]

            def wait_for(semaphore, value, gates=0):
                pool.wait_ge(gate_passed, gates + passed[0])
                pool.wait_ge(semaphore, value)
                nc.gpsimd.tensor_tensor(gate[:], ones[:, 0:2], ones[:, 0:2], ALU.add).then_inc(gate_passed, 1)
                passed[0] += 1

            def take_index(to, e, base, gates):
                copied[0] += 1
                nc.gpsimd.tensor_copy(to[:], ids[:, bass.ds(e * S, S)]).then_inc(idx_copied, 1)
                wait_for(idx_copied, base + copied[0], gates)

            def gather_x(e, q, base=0, gates=0):
                take_index(idx_x[q], e, base, gates)
                for s in range(S):
                    nc.gpsimd.indirect_dma_start(
                        out=xg[q][:, s, :], out_offset=None, in_=xrows,
                        in_offset=bass.IndirectOffsetOnAxis(ap=idx_x[q][:, s:s + 1], axis=0),
                        bounds_check=NTOK - 1, oob_is_err=False).then_inc(xg_loaded[q], 16)

            def gather_res(e, q, base=0, gates=0):
                take_index(idx_o[q], e, base, gates)
                for s in range(S):
                    nc.gpsimd.indirect_dma_start(
                        out=res[q][:, s, :], out_offset=None, in_=orows,
                        in_offset=bass.IndirectOffsetOnAxis(ap=idx_o[q][:, s:s + 1], axis=0),
                        bounds_check=NTOK - 1, oob_is_err=False).then_inc(res_loaded[q], 16)

            def scatter(q):
                for s in range(S):
                    nc.gpsimd.indirect_dma_start(
                        out=orows, out_offset=bass.IndirectOffsetOnAxis(ap=idx_o[q][:, s:s + 1], axis=0),
                        in_=res[q][:, s, :], in_offset=None, bounds_check=NTOK - 1,
                        oob_is_err=False).then_inc(res_stored[q], 16)

            gather_x(0, 0)
            gather_x(1, 1)
            pool.wait_ge(o_summed, NB * PAIRS)
            for q in range(2):
                pool.wait_ge(o_stored[q], NB // 2 * 32)
            for q in range(2):
                nc.gpsimd.memset(res[q][:], 0.0).then_inc(idx_copied, 1)
            copied[0] += 2
            for q in range(2):
                gather_res(q, q)
            with pool.Fori(0, E // 2 - 1) as i:
                base, gates = 4 * i, 10 * i
                for q in range(2):
                    e = 2 * i + q
                    wait_for(xn_ready, e + 1, gates)
                    gather_x(e + 2, q, base, gates)
                    wait_for(res_ready, e + 1, gates)
                    scatter(q)
                    wait_for(res_stored[q], S * 16 * (i + 1), gates)
                    gather_res(e + 2, q, base, gates)
            for q in range(2):
                pool.wait_ge(res_ready, E - 1 + q)
                scatter(q)

        @block.tensor
        def _(pe):
            mm = nc.tensor.matmul
            pe.wait_ge(consts_made, 10)
            pe.wait_ge(attn_w_loaded, 96)
            for oc in range(KC):
                for c in range(KC):
                    nc.tensor.transpose(bank[0][:, (oc * KC + c) * P:(oc * KC + c + 1) * P],
                                        wp[:, c, oc * P:(oc + 1) * P], ident[:])
            pe.wait_ge(b1_loaded, 16)
            nc.tensor.transpose(bank[1][:, 0:P], b1rows[:], ident[:]).then_inc(setup_pe, 1)
            pe.wait_ge(setup_dve, 1)
            for kc in range(KC):
                for oc in range(KC):
                    mm(bank[2 + kc][:, 0:C + 1], wqkv[:, KC + oc, kc * P:(kc + 1) * P], wqkv[:, oc, 0:C + 1],
                       start=(oc == 0), stop=(oc == KC - 1))
            for mc in range(KC):
                for oc in range(KC):
                    mm(bank[4][:, mc:mc + 1], wqkv[:, oc, mc * P:(mc + 1) * P], wqkv[:, KC + oc, C:C + 1],
                       start=(oc == 0), stop=(oc == KC - 1))
            for oc in range(KC):
                mm(bank[4][:, KC:KC + 1], wqkv[:, oc, C:C + 1].to_broadcast([P, P]), wqkv[:, KC + oc, C:C + 1],
                   start=(oc == 0), stop=(oc == KC - 1))
            pe.wait_ge(setup_dve, 2)
            for kc in range(KC):
                for oc in range(KC):
                    mm(bank[5][:, kc * C:(kc + 1) * C], wqkv[:, 2 * KC + oc, kc * P:(kc + 1) * P], wpT[:, oc, :],
                       start=(oc == 0), stop=(oc == KC - 1))
            for oc in range(KC):
                last = mm(bank[6][:, 0:C], wqkv[:, 2 * KC + oc, C:C + 1].to_broadcast([P, P]), wpT[:, oc, :],
                          start=(oc == 0), stop=(oc == KC - 1))
            last.then_inc(setup_pe, 1)
            pe.wait_ge(setup_dve, 3)
            pe.wait_ge(router_w_loaded, 32)

            def transposes(q, k):
                for u in range(2):
                    for c in range(KC):
                        last = nc.tensor.transpose(tr_ps[k % 2][:, (c * 2 + u) * P:(c * 2 + u + 1) * P],
                                                   z[q][:, 2 * k + u, c * P:(c + 1) * P], ident[:])
                last.then_inc(tr_done, 1)

            def gram(q, k):
                for u in range(2):
                    j = 2 * k + u
                    for c in range(KC):
                        last = mm(g_ps[c][:, 0:C + 1], z[q][:, j, c * P:(c + 1) * P], z[q][:, j, 0:C + 1],
                                  start=(j == 0), stop=(j == J - 1))
                if k == PAIRS - 1:
                    last.then_inc(g_done, 1)

            def logits(q, k):
                for u in range(2):
                    j = 2 * k + u
                    for c in range(KC):
                        last = mm(lg_ps[q][:, j * E:(j + 1) * E], zT[q][:, c, j * P:(j + 1) * P], wg[:, c, :],
                                  start=(c == 0), stop=(c == KC - 1))
                if k == PAIRS - 1:
                    last.then_inc(logits_done, 1)

            def prefix(q, b):
                pe.wait_ge(count_ready, b + 1)
                mm(lg_ps[q][:, J * E:J * E + E], tri[:], count[:, :, J - 1], start=True, stop=False)
                mm(lg_ps[q][:, J * E:J * E + E], ones[:], total[q][:], start=False, stop=True).then_inc(prefix_done, 1)

            def chain_t(pa, pb, b):
                pe.wait_ge(g_saved, b + 2)
                for c in range(KC):
                    for k in range(KC):
                        mm(pa[:, c * C:(c + 1) * C], G[:, k, c * P:(c + 1) * P], Bm[:, k, :],
                           start=(k == 0), stop=(k == KC - 1))
                for k in range(KC):
                    last = mm(pb[:, 0:C], G[:, k, C:C + 1].to_broadcast([P, P]), Bm[:, k, :],
                              start=(k == 0), stop=(k == KC - 1))
                last.then_inc(chain_done, 1)

            def chain_m(pa, pb, b):
                pe.wait_ge(chain_saved, 2 * b + 1)
                for c in range(KC):
                    for k in range(KC):
                        mm(pa[:, c * C:(c + 1) * C], AT[:, k, c * P:(c + 1) * P], Tm[:, k, :],
                           start=(k == 0), stop=(k == KC - 1))
                for k in range(KC):
                    last = mm(pb[:, 0:C], AT[:, k, C:C + 1].to_broadcast([P, P]), Tm[:, k, :],
                              start=(k == 0), stop=(k == KC - 1))
                last.then_inc(chain_done, 1)

            def out_pair(q, k):
                for u in range(2):
                    j = 2 * k + u
                    for c in range(KC):
                        last = mm(o_ps[k % 2][:, u * C:(u + 1) * C], zT[q][:, c, j * P:(j + 1) * P], M[q][:, c, :],
                                  start=(c == 0), stop=(c == KC - 1))
                last.then_inc(o_done, 1)

            with pe.Fori(0, NB // 2) as i:
                for q in range(2):
                    b = 2 * i + q
                    pe.wait_ge(z_ready, PAIRS * b + 1)
                    transposes(q, 0)
                    for k in range(PAIRS):
                        if k + 1 < PAIRS:
                            pe.wait_ge(z_ready, PAIRS * b + k + 2)
                            transposes(q, k + 1)
                        if k == 0:
                            pe.wait_ge(g_saved, b + 1)
                        gram(q, k)
                        pe.wait_ge(zT_ready, PAIRS * b + k + 1)
                        logits(q, k)
                        if q == 1 and k == 1:
                            chain_t(o_ps[0], o_ps[1], 2 * i)
                        if q == 1 and k == 3:
                            prefix(0, 2 * i)
                        if q == 1 and k == 4:
                            chain_m(o_ps[0], o_ps[1], 2 * i)
                pe.wait_ge(chain_saved, 4 * i + 2)
                for k in range(PAIRS):
                    if k >= 2:
                        pe.wait_ge(o_summed, PAIRS * 2 * i + k - 1)
                    out_pair(0, k)
                    if k == 0:
                        chain_t(tr_ps[0], tr_ps[1], 2 * i + 1)
                    if k == 2:
                        prefix(1, 2 * i + 1)
                    if k == 3:
                        chain_m(tr_ps[0], tr_ps[1], 2 * i + 1)
                pe.wait_ge(chain_saved, 4 * i + 4)
                for k in range(PAIRS):
                    pe.wait_ge(o_summed, PAIRS * (2 * i + 1) + k - 1)
                    out_pair(1, k)

            def xn_transposes(e, q):
                pe.wait_ge(xn_ready, e + 1)
                for c in range(KC):
                    for s in range(S):
                        last = nc.tensor.transpose(xt_ps[c][:, s * P:(s + 1) * P],
                                                   xn[q][:, s, c * P:(c + 1) * P], ident[:])
                    last.then_inc(xt_done, 1)

            def expert(i, q, last_one=False):
                e = 2 * i + q
                pe.wait_ge(w_lo_ready, PIECES * (e + 1))
                pe.wait_ge(xnT_lo_ready, 2 * e + 2)
                for n in range(HC):
                    if n >= 4:
                        pe.wait_ge(h_hi_ready, HC * e + n - 3)
                    cols = slice(n * P, (n + 1) * P)
                    for c in range(KC):
                        mm(h_ps[n % 4][:], w1_hi[q][:, c, cols], xnT_hi[:, c, :], start=(c == 0), stop=False)
                        mm(h_ps[n % 4][:], w1_hi[q][:, c, cols], xnT_lo[:, c, :], start=False, stop=False)
                        last = mm(h_ps[n % 4][:], w1_lo[q][:, c, cols], xnT_hi[:, c, :], start=False, stop=(c == KC - 1))
                    last.then_inc(h_done, 1)
                if not last_one:
                    xn_transposes(e + 1, 1 - q)
                for s in range(S):
                    if s % 2 == 0:
                        pe.wait_ge(y_free, 2 * e + s // 2 + 1)
                    rows = slice(s * P, (s + 1) * P)
                    y = y_ps[s // 2][:, s % 2 * C:(s % 2 + 1) * C]
                    for n in range(HC):
                        if s == 0:
                            pe.wait_ge(h_lo_ready, HC * e + n + 3)
                        mm(y, hT_hi[:, n, rows], w2_hi[q][:, n, :], start=(n == 0), stop=False)
                        mm(y, hT_hi[:, n, rows], w2_lo[q][:, n, :], start=False, stop=False)
                        last = mm(y, hT_lo[:, n, rows], w2_hi[q][:, n, :], start=False, stop=(n == HC - 1))
                    if s % 2 == 1:
                        last.then_inc(y_done, 1)

            pe.wait_ge(o_summed, NB * PAIRS)
            xn_transposes(0, 0)
            with pe.Fori(0, E // 2 - 1) as i:
                expert(i, 0)
                expert(i, 1)
            expert(E // 2 - 1, 0)
            expert(E // 2 - 1, 1, last_one=True)

        @block.scalar
        def _(act):
            def roots(q, b):
                act.wait_ge(var_ready, b + 1)
                nc.scalar.activation(stds[q][:], var2[q][:], ACT.Sqrt).then_inc(std_ready, 1)

            def save_zT(q, b, k):
                act.wait_ge(tr_done, PAIRS * b + k + 1)
                nc.scalar.activation(zT[q][:, :, 2 * k * P:(2 * k + 2) * P],
                                     tr_ps[k % 2][:].rearrange("p (c t) -> p c t", c=KC), ACT.Copy).then_inc(zT_ready, 1)

            def exps(b):
                act.wait_ge(shifted_ready, b + 1)
                nc.scalar.activation(Ex[:], D[:], ACT.Exp).then_inc(exp_ready, 1)

            with act.Fori(0, NB // 2) as i:
                roots(0, 2 * i)
                for k in range(PAIRS):
                    if k == 3:
                        roots(1, 2 * i + 1)
                    save_zT(0, 2 * i, k)
                for k in range(PAIRS):
                    save_zT(1, 2 * i + 1, k)
                    if k == 2:
                        exps(2 * i)
                exps(2 * i + 1)

            for q in range(2):
                act.wait_ge(meta_scattered[q], NB // 2 * J * 16)
            act.dma_start(rec[:].rearrange("p (e m) -> p e m", e=E),
                          table.rearrange("(e p s) m -> p e (s m)", e=E, s=S)).then_inc(rec_loaded, 16)

            def round_weights(e, q, pieces):
                for n in pieces:
                    raw, hi, _ = weight_piece(q, n)
                    if n % 2 == 0:
                        act.wait_ge(w1_loaded if n == 0 else w2_loaded, 16 * e + 16)
                    nc.scalar.activation(hi, raw, ACT.Copy).then_inc(w_hi_ready, 1)

            def round_xnT(e):
                for c in range(KC):
                    act.wait_ge(xt_done, 2 * e + c + 1)
                    nc.scalar.activation(xnT_hi[:, c, :], xt_ps[c][:], ACT.Copy).then_inc(xnT_hi_ready, 1)

            def hidden(e):
                for n in range(HC):
                    act.wait_ge(h_done, HC * e + n + 1)
                    act.wait_ge(h_lo_ready, HC * e + n + 1)
                    bias = b1T[:, bass.ds(e * HC + n, 1)]
                    nc.scalar.activation(relu[n % 2][:], h_ps[n % 4][:], ACT.Relu, bias=bias)
                    nc.scalar.activation(hT_hi[:, n, :], h_ps[n % 4][:], ACT.Relu, bias=bias).then_inc(h_hi_ready, 1)

            round_weights(0, 0, range(PIECES))
            round_xnT(0)
            for q in range(2):
                act.wait_ge(o_stored[q], NB // 2 * 32)
            with act.Fori(0, E // 2 - 1) as i:
                for q in range(2):
                    hidden(2 * i + q)
                    round_xnT(2 * i + q + 1)
                    round_weights(2 * i + q + 1, 1 - q, range(PIECES))
            hidden(E - 2)
            round_xnT(E - 1)
            round_weights(E - 1, 1, range(PIECES))
            hidden(E - 1)

        @block.vector
        def _(dve):
            v = nc.vector
            at = [0]
            start = [0]

            def link(op):
                op.then_inc(dve_chain, 1)
                at[0] += 1
                dve.wait_ge(dve_chain, start[0] + at[0])

            dve.wait_ge(attn_w_loaded, 96)
            for o in range(6):
                link(v.tensor_tensor_reduce(L[:].rearrange("p j e -> p (j e)"), wqkv[:, o, 0:C], nb_[:], 1.0, 0.0,
                                            ALU.mult, ALU.add, dots[:, o:o + 1]))
            v.tensor_tensor(wqkv[:, :, 0:C], wqkv[:, :, 0:C], nw[:].rearrange("p (a c) -> p a c", a=1).to_broadcast([P, 6, C]),
                            ALU.mult)
            link(v.memset(wqkv[:, :, C:ZW], 0.0))
            v.memset(total[0][:], 0.0)
            v.tensor_tensor(wqkv[:, :, C], dots[:], qkvb[:], ALU.add).then_inc(setup_dve, 1)
            dve.wait_ge(setup_pe, 1)
            link(v.tensor_copy(wpT[:].rearrange("p a c -> p (a c)"), bank[0][:]))
            v.tensor_copy(b1T[:], bank[1][:, 0:P]).then_inc(setup_dve, 1)
            dve.wait_ge(setup_pe, 2)
            scale = float(C) ** -0.5
            for kc in range(KC):
                v.tensor_scalar(AT[:, kc, :], bank[2 + kc][:, 0:C + 1], scale, None, ALU.mult)
            v.tensor_scalar(Acol[:], bank[4][:, 0:KC], scale, None, ALU.mult)
            v.tensor_scalar(Alast[:], bank[4][:, KC:KC + 1], scale, None, ALU.mult)
            v.tensor_scalar(Bsum[:], bank[6][:, 0:C], float(T), None, ALU.mult)
            v.tensor_copy(Blast[:], bank[6][:, 0:C])
            link(v.tensor_copy(Bm[:].rearrange("p k c -> p (k c)"), bank[5][:]))
            dve.wait_ge(consts_made, 10)
            dve.wait_ge(router_w_loaded, 32)
            v.memset(s1[:, 7, :], 0.0).then_inc(setup_dve, 1)
            v.memset(s1[:, 6, :], 0.0).then_inc(g_saved, 1)

            def stats(i, q):
                for j in range(J):
                    if j % (J // 2) == 0:
                        dve.wait_ge(x_loaded[q][j // (J // 2)], 16 * i + 16)
                    last = v.bn_stats(st[:, j, :], xs[q][:, j, :])
                link(last)
                me, mo, ve, vo = st[:, :, 1], st[:, :, 4], st[:, :, 2], st[:, :, 5]
                v.tensor_tensor(s1[:, 0, :], me, mo, ALU.add)
                v.tensor_tensor(s1[:, 1, :], me, mo, ALU.subtract)
                link(v.tensor_tensor(s1[:, 2, :], ve, vo, ALU.add))
                v.tensor_scalar(mean[q][:], s1[:, 0, :], 0.5, None, ALU.mult)
                v.tensor_tensor(s1[:, 3, :], s1[:, 1, :], s1[:, 1, :], ALU.mult)
                link(v.tensor_scalar(s1[:, 4, :], s1[:, 2, :], 1.0 / C, None, ALU.mult))
                link(v.scalar_tensor_tensor(s1[:, 5, :], s1[:, 3, :], 0.25, s1[:, 4, :], ALU.mult, ALU.add))
                link(v.tensor_scalar(var2[q][:, 0, :], s1[:, 5, :], EPS, None, ALU.add))
                v.scalar_tensor_tensor(var2[q][:, 1, :], var2[q][:, 0, :], EPS, s1[:, 5, :],
                                       ALU.mult, ALU.add).then_inc(var_ready, 1)

            def normalise(b, q):
                dve.wait_ge(std_ready, b + 1)
                link(v.reciprocal(rstd[q][:], stds[q][:]))
                for k in range(PAIRS):
                    for j in (2 * k, 2 * k + 1):
                        last = v.tensor_scalar(z[q][:, j, 0:C], xs[q][:, j, :], mean[q][:, j:j + 1],
                                               rstd[q][:, 1, j:j + 1], ALU.subtract, ALU.mult)
                    last.then_inc(z_ready, 1)
                v.tensor_tensor(s2[q][:], stds[q][:, 1, :], rstd[q][:, 0, :], ALU.mult)
                v.tensor_scalar(rp1[q][:], rstd[q][:, 0, :], 1.0, None, ALU.add)
                link(v.scalar_tensor_tensor(nmr[q][:], mean[q][:], -1.0, rstd[q][:, 0, :], ALU.mult, ALU.mult))

            def over_e(ap):
                return ap.rearrange("p (j a) -> p j a", a=1).to_broadcast([P, J, E])

            def over_j(ap):
                return ap.rearrange("p (a e) -> p a e", a=1).to_broadcast([P, J, E])

            def route_1(b, q):
                dve.wait_ge(logits_done, b + 1)
                link(v.tensor_tensor(key[:], lg_ps[q][:, 0:J * E].rearrange("p (j e) -> p j e", e=E), over_e(s2[q][:]), ALU.mult))
                link(v.tensor_tensor(L[:], key[:], over_j(bgb[:]), ALU.add))
                link(v.tensor_reduce(r1[:, 0, :], L[:], AX, ALU.max))
                v.tensor_tensor(D[:], L[:], over_e(r1[:, 0, :]), ALU.subtract).then_inc(shifted_ready, 1)
                dve.wait_ge(shifted_ready, b + 1)
                link(v.scalar_tensor_tensor(key[:], D[:], 0.0, over_j(rev[:]), ALU.is_ge, ALU.mult))
                link(v.tensor_reduce(r1[:, 1, :], key[:], AX, ALU.max))
                link(v.tensor_tensor(onehot[:].rearrange("p e j -> p j e"), over_j(rev[:]), over_e(r1[:, 1, :]), ALU.is_equal))
                v.tensor_tensor_scan(count[:].rearrange("p e j -> p (e j)"), scan_mask[:].rearrange("p e j -> p (e j)"),
                                     onehot[:].rearrange("p e j -> p (e j)"), 0.0, ALU.mult, ALU.add).then_inc(count_ready, 1)
                dve.wait_ge(count_ready, b + 1)
                v.tensor_scalar(r1[:, 2, :], r1[:, 1, :], -float(CAP), float(E * CAP - 1), ALU.mult, ALU.add)
                link(v.tensor_tensor(total[1 - q][:], total[q][:], count[:, :, J - 1], ALU.add))

            def route_2(b, q):
                dve.wait_ge(prefix_done, b + 1)
                link(v.tensor_tensor(posm[:], count[:], lg_ps[q][:, J * E:J * E + E].rearrange("p (e a) -> p e a", a=1).to_broadcast([P, E, J]), ALU.add))
                link(v.tensor_tensor(key[:].rearrange("p j e -> p e j"), posm[:], onehot[:], ALU.mult))
                link(v.tensor_reduce(r1[:, 3, :], key[:], AX, ALU.add))
                v.tensor_tensor(r1[:, 4, :], r1[:, 3, :], r1[:, 2, :], ALU.add)
                link(v.tensor_scalar(r1[:, 5, :], r1[:, 3, :], float(CAP), SKIP, ALU.is_gt, ALU.mult))
                v.tensor_tensor(dst[q][:], r1[:, 4, :], r1[:, 5, :], ALU.add)
                v.tensor_copy(meta[q][:, :, 0], token1[:, bass.ds(b * J, J)])
                v.tensor_copy(meta[q][:, :, 1], mean[q][:])
                v.tensor_copy(meta[q][:, :, 2], rstd[q][:, 0, :])
                dve.wait_ge(exp_ready, b + 1)
                link(v.tensor_reduce(r1[:, 6, :], Ex[:], AX, ALU.add))
                v.reciprocal(meta[q][:, :, 3], r1[:, 6, :]).then_inc(meta_ready, 1)

            def save_gram(b):
                dve.wait_ge(g_done, b + 1)
                v.tensor_copy(G[:, 0, :], g_ps[0][:, 0:C + 1])
                v.tensor_copy(G[:, 1, :], g_ps[1][:, 0:C + 1]).then_inc(g_saved, 1)
                dve.wait_ge(g_saved, b + 2)

            def save_t(pa, pb, b):
                dve.wait_ge(chain_done, 2 * b + 1)
                v.scalar_tensor_tensor(Tlast[:], pb[:, 0:C], 1.0, Bsum[:], ALU.mult, ALU.add)
                for c in range(KC):
                    last = v.scalar_tensor_tensor(Tm[:, c, :], Blast[:], G[:, c, C:C + 1], pa[:, c * C:(c + 1) * C],
                                                  ALU.mult, ALU.add)
                last.then_inc(chain_saved, 1)
                dve.wait_ge(chain_saved, 2 * b + 1)

            def save_m(pa, pb, b, q):
                dve.wait_ge(chain_done, 2 * b + 2)
                for c in range(KC):
                    v.scalar_tensor_tensor(M[q][:, c, :], Tlast[:], Acol[:, c:c + 1], pa[:, c * C:(c + 1) * C],
                                           ALU.mult, ALU.add)
                link(v.scalar_tensor_tensor(cb[q][:], Tlast[:], Alast[:, 0:1], pb[:, 0:C], ALU.mult, ALU.add))
                v.tensor_tensor(cb[q][:], cb[q][:], bp[:], ALU.add).then_inc(chain_saved, 1)
                dve.wait_ge(chain_saved, 2 * b + 2)

            def sum_pair(i, b, q, k):
                for u in range(2):
                    j = 2 * k + u
                    last = v.scalar_tensor_tensor(osb[q][:, j, :], xs[q][:, j, :], rp1[q][:, j:j + 1], cb[q][:],
                                                  ALU.mult, ALU.add)
                link(last)
                dve.wait_ge(o_done, PAIRS * b + k + 1)
                for u in range(2):
                    j = 2 * k + u
                    last = v.scalar_tensor_tensor(osb[q][:, j, :], o_ps[k % 2][:, u * C:(u + 1) * C], nmr[q][:, j:j + 1],
                                                  osb[q][:, j, :], ALU.add, ALU.add)
                last.then_inc(o_summed, 1)

            BODY = 56
            before = at[0]
            at[0] = 0
            with dve.Fori(0, NB // 2) as i:
                start[0] = i * BODY + before
                stats(i, 0)
                normalise(2 * i, 0)
                stats(i, 1)
                normalise(2 * i + 1, 1)
                save_gram(2 * i)
                route_1(2 * i, 0)
                save_t(o_ps[0], o_ps[1], 2 * i)
                route_2(2 * i, 0)
                save_m(o_ps[0], o_ps[1], 2 * i, 0)
                save_gram(2 * i + 1)
                sum_pair(i, 2 * i, 0, 0)
                route_1(2 * i + 1, 1)
                save_t(tr_ps[0], tr_ps[1], 2 * i + 1)
                for k in (1, 2):
                    sum_pair(i, 2 * i, 0, k)
                route_2(2 * i + 1, 1)
                sum_pair(i, 2 * i, 0, 3)
                save_m(tr_ps[0], tr_ps[1], 2 * i + 1, 1)
                for k in range(4, PAIRS):
                    sum_pair(i, 2 * i, 0, k)
                for k in range(PAIRS):
                    sum_pair(i, 2 * i + 1, 1, k)
            assert at[0] == BODY, at[0]
            start[0] = before + (NB // 2) * BODY
            at[0] = 0

            v.memset(s1[:, 6, :], 0.0).then_inc(y_free, 2)
            v.memset(s1[:, 7, :], 0.0).then_inc(h_lo_ready, 2)

            def record(e, s, m):
                return rec[:, bass.ds((e * S + s) * META + m, 1)]

            def normalise_rows(i, q, e):
                dve.wait_ge(xg_loaded[q], 16 * S * (i + 1))
                for s in range(S):
                    last = v.tensor_scalar(xn[q][:, s, :], xg[q][:, s, :], record(e, s, 1), record(e, s, 2),
                                           ALU.subtract, ALU.mult)
                last.then_inc(xn_ready, 1)

            def low(lo, value, hi):
                return v.tensor_tensor(lo, value, hi.bitcast(F32), ALU.subtract)

            def low_weights(e, q, pieces):
                for n in pieces:
                    raw, hi, lo = weight_piece(q, n)
                    dve.wait_ge(w_hi_ready, PIECES * e + n + 1)
                    low(lo, raw, hi).then_inc(w_lo_ready, 1)

            def low_xnT(e):
                for c in range(KC):
                    dve.wait_ge(xnT_hi_ready, 2 * e + c + 1)
                    low(xnT_lo[:, c, :], xt_ps[c][:], xnT_hi[:, c, :]).then_inc(xnT_lo_ready, 1)

            def low_hidden(e, n):
                dve.wait_ge(h_hi_ready, HC * e + n + 1)
                low(hT_lo[:, n, :], relu[n % 2][:], hT_hi[:, n, :]).then_inc(h_lo_ready, 1)

            def expert(i, q, last_one=False):
                e = 2 * i + q
                for n in range(HC):
                    low_hidden(e, n)
                    if n == 3 and not last_one:
                        normalise_rows(i + q, 1 - q, e + 1)
                if not last_one:
                    low_xnT(e + 1)
                dve.wait_ge(res_loaded[q], 16 * S * (i + 1))
                dve.wait_ge(b2_loaded[q], 16 * (i + 1))
                for s in range(S):
                    last = v.scalar_tensor_tensor(res[q][:, s, :], b2b[q][:], record(e, s, 3), res[q][:, s, :],
                                                  ALU.mult, ALU.add)
                link(last)
                if not last_one:
                    low_weights(e + 1, 1 - q, range(PIECES))
                for s in range(S):
                    if s % 2 == 0:
                        dve.wait_ge(y_done, 2 * e + s // 2 + 1)
                    last = v.scalar_tensor_tensor(res[q][:, s, :], y_ps[s // 2][:, s % 2 * C:(s % 2 + 1) * C],
                                                  record(e, s, 3), res[q][:, s, :], ALU.mult, ALU.add)
                    if s == 1:
                        last.then_inc(y_free, 1)
                last.then_inc(y_free, 1)
                dve.wait_ge(y_free, 2 * e + 4)
                v.memset(s1[:, 6, :], 0.0).then_inc(res_ready, 1)

            low_weights(0, 0, range(PIECES))
            normalise_rows(0, 0, 0)
            low_xnT(0)
            for q in range(2):
                dve.wait_ge(o_stored[q], NB // 2 * 32)
            base = start[0] + at[0]
            at[0] = 0
            with dve.Fori(0, E // 2 - 1) as i:
                start[0] = base + 2 * i
                expert(i, 0)
                expert(i, 1)
            assert at[0] == 2
            start[0] = base + 2 * (E // 2 - 1)
            at[0] = 0
            expert(E // 2 - 1, 0)
            expert(E // 2 - 1, 1, last_one=True)


_INS = ["L0_attn_x", "L0_attn_norm_w", "L0_attn_norm_b", "L0_attn_qkv_w", "L0_attn_qkv_b", "L0_attn_proj_w",
        "L0_attn_proj_b", "L0_ffn_Wg", "L0_ffn_bg", "L0_ffn_W1", "L0_ffn_b1", "L0_ffn_W2", "L0_ffn_b2"]


def kernel(**inputs):
    import numpy as np
    import concourse.bacc as bacc
    from concourse.bass_utils import run_bass_kernel_spmd

    nc = bacc.Bacc("TRN2", target_bir_lowering=False, num_devices=1)
    arrays, args = {}, []
    for name in _INS:
        a = np.ascontiguousarray(inputs[name])
        arrays[f"in_{name}"] = a
        args.append(nc.dram_tensor(f"in_{name}", a.shape, mybir.dt.from_np(a.dtype), kind="ExternalInput").ap())
    out = nc.dram_tensor("out", (NB, T, C), F32, kind="ExternalOutput").ap()
    program(nc, *args, out)
    r = run_bass_kernel_spmd(nc, [arrays], core_ids=[0])
    return r.results[0]["out"]
```

```python
from contextlib import ExitStack

import concourse.bass as bass
from concourse import mybir
from concourse.alu_op_type import AluOpType as ALU

ACT = mybir.ActivationFunctionType
F32 = mybir.dt.float32
F32R = mybir.dt.float32r
U32 = mybir.dt.uint32
AX = mybir.AxisListType.X

P = 128
NB = 4
T = 2048
C = 256
KC = C // P
J = T // P
JH = J // 2
PAIRS = J // 2
E = 16
H = 1024
HC = H // P
NTOK = NB * T
CAP = -(-NTOK // E)
S = CAP // P
EPS = 1e-5
ZW = C + 2
SKIP = 2.0 * NTOK
PIECES = 4
HALVES = (slice(0, J // 2), slice(J // 2, J))
WARM_UP = 20
UNITS = ((0, slice(0, J)), (1, HALVES[0]), (1, HALVES[1]))
LATE = 6
META = 4


def program(nc, x, norm_w, norm_b, qkv_w, qkv_b, proj_w, proj_b, Wg, bg, W1, b1, W2, b2, out):
    table = nc.dram_tensor("slot_records", (E * CAP, META), F32).ap()
    xrows = x.rearrange("b t c -> (b t) c")
    orows = out.rearrange("b t c -> (b t) c")

    def halves(a):
        whole = a.rearrange("b (p j) c -> b p j c", j=J)
        split = a.rearrange("b (h p j) c -> b h p j c", h=2, j=JH)
        return [[split[b, h] if b % 2 else whole[b, :, HALVES[h], :] for h in range(2)] for b in range(NB)]

    xb, ob = halves(x), halves(out)

    with ExitStack() as ctx:
        def sb(name, shape, dt=F32, stack=None):
            return (stack or ctx).enter_context(nc.sbuf_tensor(name, shape, dt))

        def sem(name):
            return ctx.enter_context(nc.semaphore(name))

        def two(name, shape, dt=F32, stack=None):
            return [sb(f"{name}{q}", shape, dt, stack) for q in range(2)]

        bank = [ctx.enter_context(nc.psum_tensor(f"bank{n}", [P, 512], F32)) for n in range(8)]
        tr_ps, g_ps, lg_ps, o_ps = bank[0:2], bank[2:4], bank[4:6], bank[6:8]
        h_ps, y_ps, xt_ps = bank[0:4], bank[4:6], bank[6:8]

        def logit_bank(u):
            return lg_ps[u % 2]

        def out_bank(k):
            return (o_ps + g_ps)[k % 4]

        def y_tile(s, last_one):
            return xt_ps[0][:, 0:C] if last_one and s == S - 1 else y_ps[s // 2][:, s % 2 * C:(s % 2 + 1) * C]

        def y_ends(s, last_one):
            return s % 2 == 1 or last_one and s == S - 2

        ident = sb("ident", [P, P])
        tri = sb("tri", [P, P])
        ones = sb("ones", [P, P])
        root1 = sb("root1", [P, 1])
        scan_mask = {w: sb(f"scan_mask{w}", [P, E * w]) for w in (J, JH)}
        rev = sb("rev", [P, E])
        token = sb("token", [P, NB * J])
        dots = sb("dots", [P, 6])
        qkvb = sb("qkvb", [P, 6])
        bp = sb("bp", [P, C])
        AT = sb("AT", [P, KC, C + 1])
        Acol = sb("Acol", [P, KC])
        Alast = sb("Alast", [P, 1])
        Bm = sb("Bm", [P, KC, C])
        Blast = sb("Blast", [P, C])
        Bsum = sb("Bsum", [P, C])
        wg = sb("wg", [P, KC, E])
        bgb = sb("bgb", [P, E])
        b1rows = sb("b1rows", [P, P])
        b1T = sb("b1T", [P, E * HC])
        G = sb("G", [P, KC, C + 1])
        Tm = sb("Tm", [P, KC, C])
        Tlast = sb("Tlast", [P, C])
        Mf = sb("Mf", [P, KC, C])
        M_hi = two("M_hi", [P, KC, C], F32R)
        M_lo = two("M_lo", [P, KC, C], F32R)
        c1 = sb("c1", [2, C])
        c_hi = sb("c_hi", [2, C], F32R)
        c_parts = two("c_parts", [2, C], F32R)
        ones_r = sb("ones_r", [2, P], F32R)
        st = sb("st", [P, J, 6])
        s1 = sb("s1", [P, 8, J])
        stds = two("stds", [P, 2, J])
        var2 = two("var2", [P, 2, J])
        mean = two("mean", [P, J])
        rstd = two("rstd", [P, 2, J])
        s2 = two("s2", [P, J])
        rp1 = two("rp1", [P, J])
        nmr = two("nmr", [P, J])
        L = sb("L", [P, J * E])
        D = sb("D", [P, J * E])
        Ex = sb("Ex", [P, J * E])
        key = sb("key", [P, J * E])
        onehot = sb("onehot", [P, E * J])
        count = sb("count", [P, E * J])
        posm = sb("posm", [P, E * J])
        r1 = sb("r1", [P, 8, J])
        total = [sb(f"total{u}", [P, E]) for u in range(len(UNITS))]
        dst = two("dst", [P, J], U32)
        meta = two("meta", [P, J, META])
        raw = ctx.enter_context(ExitStack())
        zT = sb("zT", [P, KC, T], stack=raw)
        raw.close()
        w1 = sb("w1", [P, KC, H])
        w2 = sb("w2", [P, HC, C])
        b2b = two("b2b", [P, C])
        rec = sb("rec", [P, E * S * META])
        idx_x = two("idx_x", [P, S], U32)
        idx_o = two("idx_o", [P, S], U32)
        gate = sb("gate", [P, 2])
        xg = two("xg", [P, S, C])

        early = ctx.enter_context(ExitStack())
        zT_hi = [sb("zT_hi0", [P, KC, T], F32R, early)]
        zT_lo = [sb("zT_lo0", [P, KC, T], F32R, early)]
        xs = two("xs", [P, J, C], stack=early)
        z = two("z", [P, J, ZW], stack=early)
        zT_hi.append(sb("zT_hi1", [P, KC, T], F32R, early))
        setup = ctx.enter_context(ExitStack())
        empty = sb("empty", [P, E * CAP * META // P], stack=setup)
        wqkv = sb("wqkv", [P, 6, ZW], stack=setup)
        wp = sb("wp", [P, KC, C], stack=setup)
        wpT = sb("wpT", [P, KC, C], stack=setup)
        nw = sb("nw", [P, C], stack=setup)
        nb_ = sb("nb", [P, C], stack=setup)
        setup.close()
        zT_lo.append(sb("zT_lo1", [P, KC, T], F32R, early))
        osb = [t[:, :, 0:C] for t in z]
        early.close()
        w1_hi, w1_lo, w2_hi, w2_lo = [], [], [], []

        def split_weights(q):
            w1_hi.append(sb(f"w1_hi{q}", [P, KC, H], F32R))
            w1_lo.append(sb(f"w1_lo{q}", [P, KC, H], F32R))
            w2_hi.append(sb(f"w2_hi{q}", [P, HC, C], F32R))
            w2_lo.append(sb(f"w2_lo{q}", [P, HC, C], F32R))

        split_weights(0)
        xn = two("xn", [P, S, C])
        xnT_hi = sb("xnT_hi", [P, KC, CAP], F32R)
        xnT_lo = sb("xnT_lo", [P, KC, CAP], F32R)
        hT_hi = sb("hT_hi", [P, HC, CAP], F32R)
        split_weights(1)
        res = two("res", [P, S, C])
        relu = two("relu", [P, CAP])
        hT_lo = sb("hT_lo", [P, HC, CAP], F32R)

        consts_made = sem("consts_made")
        fold_w_loaded = sem("fold_w_loaded")
        proj_w_loaded = sem("proj_w_loaded")
        router_w_loaded = sem("router_w_loaded")
        x_loaded = [[sem(f"x_loaded{q}{h}") for h in range(2)] for q in range(2)]
        table_cleared = sem("table_cleared")
        w1_loaded = sem("w1_loaded")
        w2_loaded = sem("w2_loaded")
        b2_loaded = [sem(f"b2_loaded{q}") for q in range(2)]
        w_hi_ready = sem("w_hi_ready")
        w_lo_ready = sem("w_lo_ready")
        b1_loaded = sem("b1_loaded")
        setup_pe = sem("setup_pe")
        setup_dve = sem("setup_dve")
        setup_act = sem("setup_act")
        dve_chain = sem("dve_chain")
        ahead_chain = sem("ahead_chain")
        var_ready = sem("var_ready")
        std_ready = sem("std_ready")
        z_late = sem("z_late")
        z_ready = [sem(f"z_ready{q}") for q in range(2)]
        tr_done = sem("tr_done")
        zT_ready = sem("zT_ready")
        zT_hi_ready = sem("zT_hi_ready")
        zT_lo_ready = [sem(f"zT_lo_ready{q}") for q in range(2)]
        g_done = sem("g_done")
        g_saved = sem("g_saved")
        logits_done = sem("logits_done")
        shifted_ready = sem("shifted_ready")
        exp_ready = sem("exp_ready")
        count_ready = sem("count_ready")
        prefix_done = sem("prefix_done")
        chain_done = sem("chain_done")
        chain_saved = sem("chain_saved")
        meta_ready = sem("meta_ready")
        meta_scattered = [sem(f"meta_scattered{q}") for q in range(2)]
        c_ready = sem("c_ready")
        xr_ready = sem("xr_ready")
        factors_ready = sem("factors_ready")
        o_done = sem("o_done")
        o_summed = sem("o_summed")
        o_stored = [sem(f"o_stored{q}") for q in range(2)]
        rec_loaded = sem("rec_loaded")
        idx_copied = sem("idx_copied")
        gate_passed = sem("gate_passed")
        xg_loaded = [sem(f"xg_loaded{q}") for q in range(2)]
        res_loaded = [sem(f"res_loaded{q}") for q in range(2)]
        xn_ready = sem("xn_ready")
        xt_done = sem("xt_done")
        xnT_hi_ready = sem("xnT_hi_ready")
        xnT_lo_ready = sem("xnT_lo_ready")
        h_done = sem("h_done")
        h_hi_ready = sem("h_hi_ready")
        h_lo_ready = sem("h_lo_ready")
        y_done = sem("y_done")
        y_free = sem("y_free")
        res_ready = sem("res_ready")
        res_stored = [sem(f"res_stored{q}") for q in range(2)]

        def weight_piece(q, n):
            if n < 2:
                return w1[:, n, :], w1_hi[q][:, n, :], w1_lo[q][:, n, :]
            ks = slice((n - 2) * HC // 2, (n - 1) * HC // 2)
            return w2[:, ks, :], w2_hi[q][:, ks, :], w2_lo[q][:, ks, :]

        block = ctx.enter_context(nc.Block())

        @block.sync
        def _(sp):
            def load_x(b, h):
                sp.dma_start(xs[b % 2][:, HALVES[h], :], xb[b][h]).then_inc(x_loaded[b % 2][h], 16)

            sp.dma_start(wqkv[:, :, 0:C], qkv_w.rearrange("(k p) c -> p k c", p=P)).then_inc(fold_w_loaded, 16)
            sp.dma_start(nb_[:], norm_b.rearrange("(a c) -> a c", a=1).to_broadcast([P, C])).then_inc(fold_w_loaded, 16)
            sp.dma_start(nw[:], norm_w.rearrange("(a c) -> a c", a=1).to_broadcast([P, C])).then_inc(fold_w_loaded, 16)
            with nc.allow_non_contiguous_dma(reason="768 bias values, one by one on their partitions"):
                sp.dma_start(qkvb[:], qkv_b.rearrange("(k p) -> p k", p=P)).then_inc(fold_w_loaded, 16)
            sp.dma_start(wp[:], proj_w.rearrange("(k p) c -> p k c", p=P)).then_inc(proj_w_loaded, 16)
            load_x(0, 0)
            sp.dma_start(b1rows[:], b1.rearrange("e (k p) -> (e k) p", p=P)).then_inc(b1_loaded, 16)
            load_x(0, 1)
            sp.dma_start(wg[:], Wg.rearrange("(k p) e -> p k e", p=P)).then_inc(router_w_loaded, 16)
            sp.dma_start(bgb[:], bg.rearrange("(a e) -> a e", a=1).to_broadcast([P, E])).then_inc(router_w_loaded, 16)
            sp.dma_start(bp[:], proj_b.rearrange("(a c) -> a c", a=1).to_broadcast([P, C])).then_inc(router_w_loaded, 16)
            for h in range(2):
                load_x(1, h)
            sp.wait_ge(consts_made, 2)
            sp.dma_start(table.rearrange("(p r) m -> p (r m)", p=P), empty[:]).then_inc(table_cleared, 16)

            def load_weights(e):
                sp.dma_start(w1[:], W1[bass.ds(e, 1)].rearrange("a (k p) h -> p (a k) h", p=P)).then_inc(w1_loaded, 16)
                sp.dma_start(w2[:], W2[bass.ds(e, 1)].rearrange("a (k p) c -> p (a k) c", p=P)).then_inc(w2_loaded, 16)

            def load_bias(e, q):
                sp.dma_start(b2b[q][:], b2[bass.ds(e, 1)].to_broadcast([P, C])).then_inc(b2_loaded[q], 16)

            load_bias(0, 0)
            load_bias(1, 1)
            for b in range(NB):
                if b == NB - 2:
                    sp.wait_ge(logits_done, NB // 2 * len(UNITS))
                    for q in range(2):
                        sp.wait_ge(zT_lo_ready[q], PAIRS * (NB // 2 + q))
                    load_weights(0)
                for h in range(2):
                    sp.wait_ge(o_summed, PAIRS * b + PAIRS // 2 * (h + 1) + 1)
                    sp.dma_start(ob[b][h], osb[b % 2][:, HALVES[h], :]).then_inc(o_stored[b % 2], 16)
                    if b + 2 < NB:
                        sp.wait_ge(meta_scattered[b % 2], 16 * J * (b // 2 + 1))
                        load_x(b + 2, h)
            sp.wait_ge(w_lo_ready, PIECES)
            load_weights(1)
            with sp.Fori(1, E // 2) as i:
                for q in range(2):
                    sp.wait_ge(w_lo_ready, PIECES * 2 * i + PIECES * q)
                    load_weights(2 * i + q)
                    sp.wait_ge(res_ready, 2 * i - 1 + q)
                    load_bias(2 * i + q, q)
            for q in range(2):
                sp.wait_ge(res_stored[q], E // 2 * S * 16)

        @block.gpsimd
        def _(pool):
            nc.gpsimd.memset(empty[:], 0.0).then_inc(consts_made, 1)
            pool.wait_ge(consts_made, 1)
            nc.gpsimd.memset(empty[:].rearrange("p (r m) -> p r m", m=META)[:, :, 0], SKIP).then_inc(consts_made, 1)
            nc.gpsimd.memset(ones[:], 1.0).then_inc(consts_made, 1)
            for mask in scan_mask.values():
                nc.gpsimd.memset(mask[:], 1.0).then_inc(consts_made, 1)
            nc.gpsimd.memset(z[0][:, :, C:ZW], 1.0).then_inc(consts_made, 1)
            nc.gpsimd.memset(z[1][:, :, C:ZW], 1.0).then_inc(consts_made, 1)
            nc.gpsimd.iota(rev[:], pattern=[[-1, E]], base=E, channel_multiplier=0,
                           allow_small_or_imprecise_dtypes=True).then_inc(consts_made, 1)
            tokens = token[:].rearrange("p (i q j) -> p q i j", q=2, j=J)
            nc.gpsimd.iota(tokens[:, 0], pattern=[[2 * T, NB // 2], [1, J]], base=0, channel_multiplier=J,
                           allow_small_or_imprecise_dtypes=True).then_inc(consts_made, 1)
            for h in range(2):
                nc.gpsimd.iota(tokens[:, 1, :, HALVES[h]], pattern=[[2 * T, NB // 2], [1, JH]], base=T + h * T // 2,
                               channel_multiplier=JH, allow_small_or_imprecise_dtypes=True).then_inc(consts_made, 1)
            pool.wait_ge(consts_made, 11)
            nc.gpsimd.affine_select(out=ident[:], in_=ones[:], compare_op=ALU.is_equal, fill=0.0, base=0,
                                    pattern=[[-1, P]], channel_multiplier=1).then_inc(consts_made, 1)
            nc.gpsimd.affine_select(out=tri[:], in_=ones[:], compare_op=ALU.is_gt, fill=0.0, base=0,
                                    pattern=[[1, P]], channel_multiplier=-1).then_inc(consts_made, 1)
            for w, mask in scan_mask.items():
                nc.gpsimd.memset(mask[:].rearrange("p (e j) -> p e j", j=w)[:, :, 0:1], 0.0).then_inc(consts_made, 1)
            pool.wait_ge(table_cleared, 16)
            for n in range(NB // 2 * len(UNITS)):
                b, js = UNITS[n % len(UNITS)]
                if b == 0:
                    pool.wait_ge(factors_ready, n + 2)
                    for j in range(2 * LATE, J):
                        last = nc.gpsimd.tensor_scalar(z[0][:, j, 0:C], xs[0][:, j, :], mean[0][:, j:j + 1],
                                                       rstd[0][:, 1, j:j + 1], ALU.subtract, ALU.mult)
                        if j % 2 == 1:
                            last.then_inc(z_late, 1)
                    for k in range(PAIRS):
                        columns = slice(2 * k * P, (2 * k + 2) * P)
                        pool.wait_ge(zT_hi_ready, 2 * PAIRS * (n // len(UNITS)) + k + 1)
                        nc.gpsimd.tensor_tensor(zT_lo[0][:, :, columns], zT[:, :, columns],
                                                zT_hi[0][:, :, columns].bitcast(F32), ALU.subtract).then_inc(zT_lo_ready[0], 1)
                pool.wait_ge(meta_ready, n + 1)
                for j in range(js.start, js.stop):
                    nc.gpsimd.indirect_dma_start(
                        out=table, out_offset=bass.IndirectOffsetOnAxis(ap=dst[b][:, j:j + 1], axis=0),
                        in_=meta[b][:, j, :], in_offset=None, bounds_check=E * CAP - 1,
                        oob_is_err=False).then_inc(meta_scattered[b], 16)
            for q in range(2):
                nc.gpsimd.memset(xg[q][:], 0.0).then_inc(idx_copied, 1)
            pool.wait_ge(rec_loaded, 16)
            slots = rec[:].rearrange("p (n m) -> p n m", m=META)
            copied = [2]

            passed = [0]

            def wait_for(semaphore, value, gates=0):
                pool.wait_ge(gate_passed, gates + passed[0])
                pool.wait_ge(semaphore, value)
                nc.gpsimd.tensor_tensor(gate[:], ones[:, 0:2], ones[:, 0:2], ALU.add).then_inc(gate_passed, 1)
                passed[0] += 1

            def take_index(to, e, base, gates):
                copied[0] += 1
                nc.gpsimd.tensor_copy(to[:], slots[:, bass.ds(e * S, S), 0]).then_inc(idx_copied, 1)
                wait_for(idx_copied, base + copied[0], gates)

            def gather_x(e, q, base=0, gates=0):
                take_index(idx_x[q], e, base, gates)
                for s in range(S):
                    nc.gpsimd.indirect_dma_start(
                        out=xg[q][:, s, :], out_offset=None, in_=xrows,
                        in_offset=bass.IndirectOffsetOnAxis(ap=idx_x[q][:, s:s + 1], axis=0),
                        bounds_check=NTOK - 1, oob_is_err=False).then_inc(xg_loaded[q], 16)

            def gather_res(e, q, base=0, gates=0):
                take_index(idx_o[q], e, base, gates)
                for s in range(S):
                    nc.gpsimd.indirect_dma_start(
                        out=res[q][:, s, :], out_offset=None, in_=orows,
                        in_offset=bass.IndirectOffsetOnAxis(ap=idx_o[q][:, s:s + 1], axis=0),
                        bounds_check=NTOK - 1, oob_is_err=False).then_inc(res_loaded[q], 16)

            def scatter_tile(q, s):
                nc.gpsimd.indirect_dma_start(
                    out=orows, out_offset=bass.IndirectOffsetOnAxis(ap=idx_o[q][:, s:s + 1], axis=0),
                    in_=res[q][:, s, :], in_offset=None, bounds_check=NTOK - 1,
                    oob_is_err=False).then_inc(res_stored[q], 16)

            def scatter(q):
                for s in range(S):
                    scatter_tile(q, s)

            gather_x(0, 0)
            gather_x(1, 1)
            pool.wait_ge(o_summed, NB * PAIRS + 1)
            for q in range(2):
                pool.wait_ge(o_stored[q], NB // 2 * 32 + 1)
            for q in range(2):
                nc.gpsimd.memset(res[q][:], 0.0).then_inc(idx_copied, 1)
            copied[0] += 2
            for q in range(2):
                gather_res(q, q)
            with pool.Fori(0, E // 2 - 1) as i:
                base, gates = 4 * i, 10 * i
                for q in range(2):
                    e = 2 * i + q
                    wait_for(xn_ready, e + 1, gates)
                    gather_x(e + 2, q, base, gates)
                    wait_for(res_ready, e + 1, gates)
                    scatter(q)
                    wait_for(res_stored[q], S * 16 * (i + 1), gates)
                    gather_res(e + 2, q, base, gates)
            pool.wait_ge(res_ready, E - 1)
            scatter(0)
            banks = 0
            for s in range(S):
                if s == 0 or y_ends(s - 1, True):
                    banks += 1
                    pool.wait_ge(y_free, 2 * (E - 1) + 2 + banks)
                scatter_tile(1, s)

        @block.tensor
        def _(pe):
            mm = nc.tensor.matmul
            pe.wait_ge(consts_made, 15)
            for _ in range(WARM_UP):
                mm(bank[7][:, 0:P], tri[:], ones[:], start=True, stop=True)
            pe.wait_ge(proj_w_loaded, 16)
            for oc in range(KC):
                for c in range(KC):
                    nc.tensor.transpose(bank[0][:, (oc * KC + c) * P:(oc * KC + c + 1) * P],
                                        wp[:, c, oc * P:(oc + 1) * P], ident[:])
            pe.wait_ge(b1_loaded, 16)
            nc.tensor.transpose(bank[1][:, 0:P], b1rows[:], ident[:]).then_inc(setup_pe, 1)
            pe.wait_ge(setup_dve, 1)
            for kc in range(KC):
                for oc in range(KC):
                    mm(bank[2 + kc][:, 0:C + 1], wqkv[:, KC + oc, kc * P:(kc + 1) * P], wqkv[:, oc, 0:C + 1],
                       start=(oc == 0), stop=(oc == KC - 1))
            for mc in range(KC):
                for oc in range(KC):
                    mm(bank[4][:, mc:mc + 1], wqkv[:, oc, mc * P:(mc + 1) * P], wqkv[:, KC + oc, C:C + 1],
                       start=(oc == 0), stop=(oc == KC - 1))
            for oc in range(KC):
                mm(bank[4][:, KC:KC + 1], wqkv[:, oc, C:C + 1].to_broadcast([P, P]), wqkv[:, KC + oc, C:C + 1],
                   start=(oc == 0), stop=(oc == KC - 1))
            pe.wait_ge(setup_act, 3)
            for kc in range(KC):
                for oc in range(KC):
                    mm(bank[5][:, kc * C:(kc + 1) * C], wqkv[:, 2 * KC + oc, kc * P:(kc + 1) * P], wpT[:, oc, :],
                       start=(oc == 0), stop=(oc == KC - 1))
            for oc in range(KC):
                last = mm(bank[6][:, 0:C], wqkv[:, 2 * KC + oc, C:C + 1].to_broadcast([P, P]), wpT[:, oc, :],
                          start=(oc == 0), stop=(oc == KC - 1))
            last.then_inc(setup_pe, 1)
            pe.wait_ge(router_w_loaded, 48)

            def transposes(q, k):
                for u in range(2):
                    for c in range(KC):
                        last = nc.tensor.transpose(tr_ps[k % 2][:, (c * 2 + u) * P:(c * 2 + u + 1) * P],
                                                   z[q][:, 2 * k + u, c * P:(c + 1) * P], ident[:])
                last.then_inc(tr_done, 1)

            def gram(q, k):
                for u in range(2):
                    j = 2 * k + u
                    for c in range(KC):
                        last = mm(g_ps[c][:, c * P:C + 1], z[q][:, j, c * P:(c + 1) * P], z[q][:, j, c * P:C + 1],
                                  start=(j == 0), stop=(j == J - 1))
                if k == PAIRS - 1:
                    last.then_inc(g_done, 1)

            def logits(q, k):
                unit_bank, j0 = logit_bank(q + k // (PAIRS // 2) if q else 0), JH if q and k >= PAIRS // 2 else 0
                for u in range(2):
                    j = 2 * k + u
                    for c in range(KC):
                        last = mm(unit_bank[:, (j - j0) * E:(j - j0 + 1) * E], zT[:, c, j * P:(j + 1) * P], wg[:, c, :],
                                  start=(c == 0), stop=(c == KC - 1))
                if k == PAIRS - 1 or q == 1 and k == PAIRS // 2 - 1:
                    last.then_inc(logits_done, 1)

            def prefix(i, u):
                pe.wait_ge(count_ready, len(UNITS) * i + u + 1)
                w = UNITS[u][1].stop - UNITS[u][1].start
                sums = logit_bank(u)[:, w * E:(w + 1) * E]
                mm(sums, tri[:], count[:, w - 1:w * E:w], start=True, stop=False)
                mm(sums, ones[:], total[u][:], start=False, stop=True).then_inc(prefix_done, 1)

            def chain_g(pb, b):
                pe.wait_ge(g_saved, b + 2)
                nc.tensor.transpose(pb[:, C:C + P], G[:, 0, P:C], ident[:]).then_inc(chain_done, 1)

            def chain_t(pa, pb, b):
                pe.wait_ge(chain_saved, 3 * b + 1)
                for c in range(KC):
                    for k in range(KC):
                        mm(pa[:, c * C:(c + 1) * C], G[:, k, c * P:(c + 1) * P], Bm[:, k, :],
                           start=(k == 0), stop=(k == KC - 1))
                for k in range(KC):
                    last = mm(pb[:, 0:C], G[:, k, C:C + 1].to_broadcast([P, P]), Bm[:, k, :],
                              start=(k == 0), stop=(k == KC - 1))
                last.then_inc(chain_done, 1)

            def chain_m(pa, pb, b):
                pe.wait_ge(chain_saved, 3 * b + 2)
                for c in range(KC):
                    for k in range(KC):
                        mm(pa[:, c * C:(c + 1) * C], AT[:, k, c * P:(c + 1) * P], Tm[:, k, :],
                           start=(k == 0), stop=(k == KC - 1))
                for k in range(KC):
                    last = mm(pb[:, 0:C], AT[:, k, C:C + 1].to_broadcast([P, P]), Tm[:, k, :],
                              start=(k == 0), stop=(k == KC - 1))
                last.then_inc(chain_done, 1)

            def out_pair(b, q, k):
                for u in range(2):
                    j = 2 * k + u
                    y = out_bank(k)[:, u * C:(u + 1) * C]
                    rows = slice(j * P, (j + 1) * P)
                    for c in range(KC):
                        mm(y, zT_hi[q][:, c, rows], M_hi[q][:, c, :], start=(c == 0), stop=False)
                        mm(y, zT_hi[q][:, c, rows], M_lo[q][:, c, :], start=False, stop=False)
                        mm(y, zT_lo[q][:, c, rows], M_hi[q][:, c, :], start=False, stop=False)
                    if k == 0 and u == 0:
                        pe.wait_ge(c_ready, b + 1)
                    last = mm(y, ones_r[:], c_parts[q][:], start=False, stop=True)
                last.then_inc(o_done, 1)

            with pe.Fori(0, NB // 2) as i:
                for q in range(2):
                    b = 2 * i + q
                    pe.wait_ge(z_ready[q], (PAIRS if q else LATE) * i + 1)
                    if q == 1:
                        pe.wait_ge(zT_hi_ready, PAIRS * b - 1)
                    transposes(q, 0)
                    for k in range(PAIRS):
                        if k + 1 < PAIRS:
                            if q == 0 and k + 1 >= LATE:
                                pe.wait_ge(z_late, (PAIRS - LATE) * i + k + 2 - LATE)
                            elif q == 0:
                                pe.wait_ge(z_ready[0], LATE * i + k + 2)
                            else:
                                pe.wait_ge(z_ready[1], PAIRS * i + k + 2)
                            if q == 1 or k >= 1:
                                pe.wait_ge(zT_hi_ready, PAIRS * b + k)
                            transposes(q, k + 1)
                        if k == 0:
                            pe.wait_ge(g_saved, b + 1)
                            if q == 0:
                                pe.wait_ge(o_summed, 2 * PAIRS * i + 1)
                        gram(q, k)
                        pe.wait_ge(zT_ready, PAIRS * b + k + 1)
                        if q == 1 and k == PAIRS // 2:
                            pe.wait_ge(meta_ready, len(UNITS) * i + 1)
                        logits(q, k)
                        if q == 1:
                            if k == 0:
                                chain_g(o_ps[1], 2 * i)
                            if k == 1:
                                prefix(i, 0)
                                chain_t(o_ps[0], o_ps[1], 2 * i)
                            if k == 4:
                                chain_m(o_ps[0], o_ps[1], 2 * i)
                                prefix(i, 1)
                pe.wait_ge(chain_saved, 6 * i + 3)
                pe.wait_ge(zT_lo_ready[0], PAIRS * i + PAIRS)
                for k in range(PAIRS):
                    if k == 2:
                        pe.wait_ge(g_saved, 2 * i + 3)
                    if k >= 4:
                        pe.wait_ge(o_summed, PAIRS * 2 * i + k - 2)
                    out_pair(2 * i, 0, k)
                    if k == 0:
                        pe.wait_ge(zT_hi_ready, PAIRS * (2 * i + 2))
                        chain_g(tr_ps[1], 2 * i + 1)
                    if k == 1:
                        prefix(i, 2)
                    if k == 2:
                        chain_t(tr_ps[0], tr_ps[1], 2 * i + 1)
                    if k == 4:
                        chain_m(tr_ps[0], tr_ps[1], 2 * i + 1)
                pe.wait_ge(chain_saved, 6 * i + 6)
                pe.wait_ge(zT_lo_ready[1], PAIRS * i + 2 * PAIRS)
                for k in range(PAIRS):
                    pe.wait_ge(o_summed, PAIRS * (2 * i + 1) + k - 2)
                    out_pair(2 * i + 1, 1, k)

            def xn_transposes(e, q):
                pe.wait_ge(xn_ready, e + 1)
                for c in range(KC):
                    for s in range(S):
                        last = nc.tensor.transpose(xt_ps[c][:, s * P:(s + 1) * P],
                                                   xn[q][:, s, c * P:(c + 1) * P], ident[:])
                    last.then_inc(xt_done, 1)

            def expert(i, q, last_one=False):
                e = 2 * i + q
                pe.wait_ge(w_lo_ready, PIECES * e + PIECES // 2)
                pe.wait_ge(xnT_lo_ready, 2 * e + 2)
                for n in range(HC):
                    if n >= 4:
                        pe.wait_ge(h_hi_ready, HC * e + n - 3)
                    cols = slice(n * P, (n + 1) * P)
                    for c in range(KC):
                        mm(h_ps[n % 4][:], w1_hi[q][:, c, cols], xnT_hi[:, c, :], start=(c == 0), stop=False)
                        mm(h_ps[n % 4][:], w1_hi[q][:, c, cols], xnT_lo[:, c, :], start=False, stop=False)
                        last = mm(h_ps[n % 4][:], w1_lo[q][:, c, cols], xnT_hi[:, c, :], start=False, stop=(c == KC - 1))
                    last.then_inc(h_done, 1)
                if not last_one:
                    xn_transposes(e + 1, 1 - q)
                pe.wait_ge(w_lo_ready, PIECES * e + PIECES)
                for s in range(S):
                    if s % 2 == 0:
                        pe.wait_ge(y_free, 2 * e + s // 2 + 1)
                    rows = slice(s * P, (s + 1) * P)
                    y = y_tile(s, last_one)
                    for n in range(HC):
                        if s == 0:
                            pe.wait_ge(h_lo_ready, HC * e + n + 3)
                        mm(y, hT_hi[:, n, rows], w2_hi[q][:, n, :], start=(n == 0), stop=False)
                        mm(y, hT_hi[:, n, rows], w2_lo[q][:, n, :], start=False, stop=False)
                        last = mm(y, hT_lo[:, n, rows], w2_hi[q][:, n, :], start=False, stop=(n == HC - 1))
                    if y_ends(s, last_one):
                        last.then_inc(y_done, 1)

            pe.wait_ge(o_summed, NB * PAIRS - 1)
            xn_transposes(0, 0)
            pe.wait_ge(o_summed, NB * PAIRS + 1)
            with pe.Fori(0, E // 2 - 1) as i:
                expert(i, 0)
                expert(i, 1)
            expert(E // 2 - 1, 0)
            expert(E // 2 - 1, 1, last_one=True)

        @block.scalar
        def _(act):
            act.wait_ge(consts_made, 15)
            nc.scalar.activation(root1[:], ones[:, 0:1], ACT.Sqrt)
            nc.scalar.activation(ones_r[:], ones[0:2, :], ACT.Copy).then_inc(setup_act, 1)
            act.wait_ge(setup_pe, 1)
            nc.scalar.activation(wpT[:].rearrange("p a c -> p (a c)"), bank[0][:], ACT.Copy).then_inc(setup_act, 1)
            nc.scalar.activation(b1T[:], bank[1][:, 0:P], ACT.Copy).then_inc(setup_act, 1)
            def roots(q, n, js):
                act.wait_ge(var_ready, n)
                nc.scalar.activation(stds[q][:, :, js], var2[q][:, :, js], ACT.Sqrt).then_inc(std_ready, 1)

            roots(0, 1, HALVES[0])
            act.wait_ge(setup_pe, 2)
            scale = float(C) ** -0.5
            for kc in range(KC):
                nc.scalar.activation(AT[:, kc, :], bank[2 + kc][:, 0:C + 1], ACT.Copy, scale=scale)
            nc.scalar.activation(Acol[:], bank[4][:, 0:KC], ACT.Copy, scale=scale)
            nc.scalar.activation(Alast[:], bank[4][:, KC:KC + 1], ACT.Copy, scale=scale).then_inc(g_saved, 1)
            nc.scalar.activation(Bsum[:], bank[6][:, 0:C], ACT.Copy, scale=float(T))
            nc.scalar.activation(Blast[:], bank[6][:, 0:C], ACT.Copy)
            nc.scalar.activation(Bm[:].rearrange("p k c -> p (k c)"), bank[5][:], ACT.Copy)

            def add_xn(q, k):
                for u in range(2):
                    j = 2 * k + u
                    last = nc.scalar.activation(xs[q][:, j, :], xs[q][:, j, :], ACT.Identity,
                                                bias=nmr[q][:, j:j + 1], scale=rp1[q][:, j:j + 1])
                last.then_inc(xr_ready, 1)

            def save_zT(q, i, k):
                act.wait_ge(tr_done, PAIRS * (2 * i + q) + k + 1)
                act.wait_ge(zT_lo_ready[1 - q], PAIRS * i + k + 1)
                columns = slice(2 * k * P, (2 * k + 2) * P)
                pair = tr_ps[k % 2][:].rearrange("p (c t) -> p c t", c=KC)
                nc.scalar.activation(zT[:, :, columns], pair, ACT.Copy).then_inc(zT_ready, 1)
                nc.scalar.activation(zT_hi[q][:, :, columns], pair, ACT.Copy).then_inc(zT_hi_ready, 1)

            def exps(i, u):
                act.wait_ge(shifted_ready, len(UNITS) * i + u + 1)
                columns = slice(0, (UNITS[u][1].stop - UNITS[u][1].start) * E)
                nc.scalar.activation(Ex[:, columns], D[:, columns], ACT.Exp).then_inc(exp_ready, 1)

            with act.Fori(0, NB // 2) as i:
                nc.scalar.activation(root1[:], ones[:, 0:1], ACT.Sqrt)
                for k in range(PAIRS):
                    if k == 3:
                        roots(0, 3 * i + 2, HALVES[1])
                    if k == 6:
                        roots(1, 3 * i + 3, slice(0, J))
                    save_zT(0, i, k)
                for k in range(PAIRS):
                    save_zT(1, i, k)
                    if k == 0:
                        act.wait_ge(factors_ready, 3 * i + 2)
                        act.wait_ge(z_ready[0], LATE * (i + 1))
                        act.wait_ge(z_late, (PAIRS - LATE) * (i + 1))
                    add_xn(0, k)
                    if k == 1:
                        exps(i, 0)
                    if k == 5:
                        exps(i, 1)
                exps(i, 2)
                act.wait_ge(factors_ready, 3 * i + 3)
                act.wait_ge(z_ready[1], PAIRS * i + PAIRS)
                for k in range(PAIRS):
                    add_xn(1, k)
                with act.If(i < NB // 2 - 1):
                    roots(0, 3 * i + 4, HALVES[0])

            for q in range(2):
                act.wait_ge(meta_scattered[q], NB // 2 * J * 16)
            act.dma_start(rec[:].rearrange("p (e m) -> p e m", e=E),
                          table.rearrange("(e p s) m -> p e (s m)", e=E, s=S)).then_inc(rec_loaded, 16)

            def round_weights(e, q, pieces):
                for n in pieces:
                    raw, hi, _ = weight_piece(q, n)
                    if n % 2 == 0:
                        act.wait_ge(w1_loaded if n == 0 else w2_loaded, 16 * e + 16)
                    nc.scalar.activation(hi, raw, ACT.Copy).then_inc(w_hi_ready, 1)

            def round_xnT(e):
                for c in range(KC):
                    act.wait_ge(xt_done, 2 * e + c + 1)
                    nc.scalar.activation(xnT_hi[:, c, :], xt_ps[c][:], ACT.Copy).then_inc(xnT_hi_ready, 1)

            def hidden(e):
                for n in range(HC):
                    act.wait_ge(h_done, HC * e + n + 1)
                    act.wait_ge(h_lo_ready, HC * e + n + 1)
                    bias = b1T[:, bass.ds(e * HC + n, 1)]
                    nc.scalar.activation(relu[n % 2][:], h_ps[n % 4][:], ACT.Relu, bias=bias)
                    nc.scalar.activation(hT_hi[:, n, :], h_ps[n % 4][:], ACT.Relu, bias=bias).then_inc(h_hi_ready, 1)

            act.wait_ge(o_done, PAIRS * (NB - 1))
            round_weights(0, 0, range(PIECES))
            round_xnT(0)
            for q in range(2):
                act.wait_ge(o_stored[q], NB // 2 * 32 + 1)
            with act.Fori(0, E // 2 - 1) as i:
                for q in range(2):
                    hidden(2 * i + q)
                    round_xnT(2 * i + q + 1)
                    round_weights(2 * i + q + 1, 1 - q, range(PIECES))
            hidden(E - 2)
            round_xnT(E - 1)
            round_weights(E - 1, 1, range(PIECES))
            hidden(E - 1)

        @block.vector
        def _(dve):
            v = nc.vector
            at = [0]
            start = [0]
            chain = [dve_chain]

            def link(op):
                op.then_inc(chain[0], 1)
                at[0] += 1
                dve.wait_ge(chain[0], start[0] + at[0])

            dve.wait_ge(fold_w_loaded, 64)
            for o in range(6):
                link(v.tensor_tensor_reduce(L[:], wqkv[:, o, 0:C], nb_[:], 1.0, 0.0,
                                            ALU.mult, ALU.add, dots[:, o:o + 1]))
            v.tensor_tensor(wqkv[:, :, 0:C], wqkv[:, :, 0:C], nw[:].rearrange("p (a c) -> p a c", a=1).to_broadcast([P, 6, C]),
                            ALU.mult)
            link(v.memset(wqkv[:, :, C:ZW], 0.0))
            v.memset(total[0][:], 0.0)
            v.tensor_tensor(wqkv[:, :, C], dots[:], qkvb[:], ALU.add).then_inc(setup_dve, 1)
            v.memset(s1[:, 7, :], 0.0).then_inc(o_summed, 1)
            v.memset(r1[:, 5, :], 0.0).then_inc(zT_lo_ready[1], PAIRS)
            for q in range(2):
                v.memset(r1[:, 6 + q, :], 0.0).then_inc(o_stored[q], 1)
            dve.wait_ge(consts_made, 15)
            dve.wait_ge(router_w_loaded, 48)

            def stats(i, q, h):
                dve.wait_ge(x_loaded[q][h], 16 * i + 16)
                for j in range(HALVES[h].start, HALVES[h].stop):
                    last = v.bn_stats(st[:, j, :], xs[q][:, j, :])
                link(last)

            def variances(q, js):
                me, mo, ve, vo = st[:, js, 1], st[:, js, 4], st[:, js, 2], st[:, js, 5]
                v.tensor_tensor(s1[:, 0, js], me, mo, ALU.add)
                v.tensor_tensor(s1[:, 1, js], me, mo, ALU.subtract)
                link(v.tensor_tensor(s1[:, 2, js], ve, vo, ALU.add))
                v.tensor_scalar(mean[q][:, js], s1[:, 0, js], 0.5, None, ALU.mult)
                v.tensor_tensor(s1[:, 3, js], s1[:, 1, js], s1[:, 1, js], ALU.mult)
                link(v.tensor_scalar(s1[:, 4, js], s1[:, 2, js], 1.0 / C, None, ALU.mult))
                link(v.scalar_tensor_tensor(s1[:, 5, js], s1[:, 3, js], 0.25, s1[:, 4, js], ALU.mult, ALU.add))
                link(v.tensor_scalar(var2[q][:, 0, js], s1[:, 5, js], EPS, None, ALU.add))
                v.scalar_tensor_tensor(var2[q][:, 1, js], var2[q][:, 0, js], EPS, s1[:, 5, js],
                                       ALU.mult, ALU.add).then_inc(var_ready, 1)

            def scales(q, n, js):
                dve.wait_ge(std_ready, n)
                link(v.reciprocal(rstd[q][:, :, js], stds[q][:, :, js]))

            def normalise(q, js):
                for j in range(js.start, js.stop):
                    last = v.tensor_scalar(z[q][:, j, 0:C], xs[q][:, j, :], mean[q][:, j:j + 1],
                                           rstd[q][:, 1, j:j + 1], ALU.subtract, ALU.mult)
                    if j % 2 == 1:
                        last.then_inc(z_ready[q], 1)

            def factors(q, js):
                v.tensor_tensor(s2[q][:, js], stds[q][:, 1, js], rstd[q][:, 0, js], ALU.mult)
                v.tensor_scalar(rp1[q][:, js], rstd[q][:, 0, js], 1.0, None, ALU.add)
                v.scalar_tensor_tensor(nmr[q][:, js], mean[q][:, js], -1.0, rstd[q][:, 0, js],
                                       ALU.mult, ALU.mult).then_inc(factors_ready, 1)

            def low_zT(i, ks):
                for k in ks:
                    columns = slice(2 * k * P, (2 * k + 2) * P)
                    dve.wait_ge(zT_hi_ready, PAIRS * (2 * i + 1) + k + 1)
                    v.tensor_tensor(zT_lo[1][:, :, columns], zT[:, :, columns], zT_hi[1][:, :, columns].bitcast(F32),
                                    ALU.subtract).then_inc(zT_lo_ready[1], 1)

            def views(u):
                w = UNITS[u][1].stop - UNITS[u][1].start

                def je(t):
                    return t[:, 0:w * E].rearrange("p (j e) -> p j e", e=E)

                def ej(t):
                    return t[:, 0:w * E].rearrange("p (e j) -> p e j", j=w)

                def over_e(ap):
                    return ap.rearrange("p (j a) -> p j a", a=1).to_broadcast([P, w, E])

                def over_j(ap):
                    return ap.rearrange("p (a e) -> p a e", a=1).to_broadcast([P, w, E])

                return w, je, ej, over_e, over_j

            def route_1(i, u):
                q, js = UNITS[u]
                w, je, ej, over_e, over_j = views(u)
                dve.wait_ge(logits_done, len(UNITS) * i + u + 1)
                dve.wait_ge(factors_ready, 3 * i + 2 + q)
                link(v.tensor_tensor(je(key), je(logit_bank(u)), over_e(s2[q][:, js]), ALU.mult))
                link(v.tensor_tensor(je(L), je(key), over_j(bgb[:]), ALU.add))
                link(v.tensor_reduce(r1[:, 0, 0:w], je(L), AX, ALU.max))
                v.tensor_tensor(je(D), je(L), over_e(r1[:, 0, 0:w]), ALU.subtract).then_inc(shifted_ready, 1)
                dve.wait_ge(shifted_ready, len(UNITS) * i + u + 1)
                link(v.scalar_tensor_tensor(je(key), je(D), 0.0, over_j(rev[:]), ALU.is_ge, ALU.mult))
                link(v.tensor_reduce(r1[:, 1, 0:w], je(key), AX, ALU.max))
                link(v.tensor_tensor(ej(onehot).rearrange("p e j -> p j e"), over_j(rev[:]), over_e(r1[:, 1, 0:w]), ALU.is_equal))
                v.tensor_tensor_scan(count[:, 0:w * E], scan_mask[w][:], onehot[:, 0:w * E], 0.0,
                                     ALU.mult, ALU.add).then_inc(count_ready, 1)
                dve.wait_ge(count_ready, len(UNITS) * i + u + 1)
                v.tensor_scalar(r1[:, 2, 0:w], r1[:, 1, 0:w], -float(CAP), float(E * CAP - 1), ALU.mult, ALU.add)
                link(v.tensor_tensor(total[(u + 1) % len(UNITS)][:], total[u][:], count[:, w - 1:w * E:w], ALU.add))

            def route_2(i, u):
                q, js = UNITS[u]
                w, je, ej, over_e, over_j = views(u)
                dve.wait_ge(prefix_done, len(UNITS) * i + u + 1)
                lower = logit_bank(u)[:, w * E:(w + 1) * E].rearrange("p (e a) -> p e a", a=1).to_broadcast([P, E, w])
                link(v.tensor_tensor(ej(posm), ej(count), lower, ALU.add))
                link(v.tensor_tensor(je(key).rearrange("p j e -> p e j"), ej(posm), ej(onehot), ALU.mult))
                link(v.tensor_reduce(r1[:, 3, 0:w], je(key), AX, ALU.add))
                v.tensor_tensor(r1[:, 4, 0:w], r1[:, 3, 0:w], r1[:, 2, 0:w], ALU.add)
                link(v.tensor_scalar(r1[:, 5, 0:w], r1[:, 3, 0:w], float(CAP), SKIP, ALU.is_gt, ALU.mult))
                v.tensor_tensor(dst[q][:, js], r1[:, 4, 0:w], r1[:, 5, 0:w], ALU.add)
                v.tensor_copy(meta[q][:, js, 0], token[:, bass.ds((2 * i + q) * J + js.start, w)])
                v.tensor_copy(meta[q][:, js, 1], mean[q][:, js])
                v.tensor_copy(meta[q][:, js, 2], rstd[q][:, 0, js])
                dve.wait_ge(exp_ready, len(UNITS) * i + u + 1)
                link(v.tensor_reduce(r1[:, 6, 0:w], je(Ex), AX, ALU.add))
                v.reciprocal(meta[q][:, js, 3], r1[:, 6, 0:w]).then_inc(meta_ready, 1)

            def save_gram(b):
                dve.wait_ge(g_done, b + 1)
                v.tensor_copy(G[:, 0, :], g_ps[0][:, 0:C + 1])
                v.tensor_copy(G[:, 1, P:C + 1], g_ps[1][:, P:C + 1]).then_inc(g_saved, 1)

            def save_mirror(pb, b):
                dve.wait_ge(chain_done, 3 * b + 1)
                v.tensor_copy(G[:, 1, 0:P], pb[:, C:C + P]).then_inc(chain_saved, 1)

            def save_t(pa, pb, b):
                dve.wait_ge(chain_done, 3 * b + 2)
                v.scalar_tensor_tensor(Tlast[:], pb[:, 0:C], 1.0, Bsum[:], ALU.mult, ALU.add)
                for c in range(KC):
                    last = v.scalar_tensor_tensor(Tm[:, c, :], Blast[:], G[:, c, C:C + 1], pa[:, c * C:(c + 1) * C],
                                                  ALU.mult, ALU.add)
                last.then_inc(chain_saved, 1)
                dve.wait_ge(chain_saved, 3 * b + 2)

            def save_m(pa, pb, b, q):
                dve.wait_ge(chain_done, 3 * b + 3)
                for c in range(KC):
                    last = v.scalar_tensor_tensor(Mf[:, c, :], Tlast[:], Acol[:, c:c + 1], pa[:, c * C:(c + 1) * C],
                                                  ALU.mult, ALU.add)
                link(last)
                link(v.tensor_copy(M_hi[q][:], Mf[:]))
                v.tensor_tensor(M_lo[q][:], Mf[:], M_hi[q][:].bitcast(F32), ALU.subtract).then_inc(chain_saved, 1)
                link(v.scalar_tensor_tensor(c1[:], Tlast[0:2, :], Alast[0:2, 0:1], pb[0:2, 0:C], ALU.mult, ALU.add))
                link(v.tensor_tensor(c1[:], c1[:], bp[0:2, :], ALU.add))
                link(v.tensor_copy(c_hi[:], c1[:]))
                link(v.tensor_tensor(c_parts[q][:], c1[:], c_hi[:].bitcast(F32), ALU.subtract))
                v.tensor_copy(c_parts[q][0:1, :], c_hi[0:1, :].bitcast(F32)).then_inc(c_ready, 1)

            def sum_pair(b, q, k):
                dve.wait_ge(xr_ready, PAIRS * b + k + 1)
                dve.wait_ge(o_done, PAIRS * b + k + 1)
                v.tensor_tensor(osb[q][:, 2 * k:2 * k + 2, :], xs[q][:, 2 * k:2 * k + 2, :],
                                out_bank(k)[:].rearrange("p (j c) -> p j c", c=C), ALU.add).then_inc(o_summed, 1)

            stats(0, 0, 0)
            variances(0, HALVES[0])
            scales(0, 1, HALVES[0])
            normalise(0, HALVES[0])
            stats(0, 0, 1)
            variances(0, HALVES[1])
            factors(0, HALVES[0])

            def record(e, s, m):
                return rec[:, bass.ds((e * S + s) * META + m, 1)]

            def normalise_rows(i, q, e):
                dve.wait_ge(xg_loaded[q], 16 * S * (i + 1))
                for s in range(S):
                    last = v.tensor_scalar(xn[q][:, s, :], xg[q][:, s, :], record(e, s, 1), record(e, s, 2),
                                           ALU.subtract, ALU.mult)
                last.then_inc(xn_ready, 1)

            def low(lo, value, hi):
                return v.tensor_tensor(lo, value, hi.bitcast(F32), ALU.subtract)

            def low_weights(e, q, pieces):
                for n in pieces:
                    raw, hi, lo = weight_piece(q, n)
                    dve.wait_ge(w_hi_ready, PIECES * e + n + 1)
                    low(lo, raw, hi).then_inc(w_lo_ready, 1)

            BODY = 56
            AHEAD = {1: 5, 3: 1, PAIRS - 1: 5}
            AHEAD_STEPS = sum(AHEAD.values())
            dve.wait_ge(table_cleared, 16)
            before = at[0]
            at[0] = 0
            with dve.Fori(0, NB // 2) as i:
                start[0] = i * BODY + before
                scales(0, 3 * i + 2, HALVES[1])
                factors(0, HALVES[1])
                normalise(0, slice(JH, 2 * LATE))
                stats(i, 1, 0)
                stats(i, 1, 1)
                variances(1, slice(0, J))
                scales(1, 3 * i + 3, slice(0, J))
                dve.wait_ge(o_stored[1], 32 * i + 1)
                normalise(1, slice(0, J))
                factors(1, slice(0, J))
                save_gram(2 * i)
                route_1(i, 0)
                save_mirror(o_ps[1], 2 * i)
                route_2(i, 0)
                low_zT(i, (0, 1))
                save_t(o_ps[0], o_ps[1], 2 * i)
                low_zT(i, (2, 3))
                route_1(i, 1)
                low_zT(i, (4,))
                route_2(i, 1)
                low_zT(i, (5,))
                save_m(o_ps[0], o_ps[1], 2 * i, 0)
                low_zT(i, (6,))
                save_gram(2 * i + 1)
                route_1(i, 2)
                low_zT(i, (7,))
                save_mirror(tr_ps[1], 2 * i + 1)
                route_2(i, 2)
                sum_pair(2 * i, 0, 0)
                sum_pair(2 * i, 0, 1)
                save_t(tr_ps[0], tr_ps[1], 2 * i + 1)
                for k in range(2, 5):
                    sum_pair(2 * i, 0, k)
                save_m(tr_ps[0], tr_ps[1], 2 * i + 1, 1)
                for k in range(5, PAIRS):
                    sum_pair(2 * i, 0, k)
                for k in range(PAIRS):
                    sum_pair(2 * i + 1, 1, k)
                    if k in AHEAD:
                        order, chain[0] = (chain[0], start[0], at[0]), ahead_chain
                        start[0], at[0] = i * AHEAD_STEPS + sum(n for m, n in AHEAD.items() if m < k), 0
                        with dve.If(i < NB // 2 - 1):
                            if k == 3:
                                dve.wait_ge(o_stored[0], 32 * i + 33)
                                scales(0, 3 * i + 4, HALVES[0])
                                normalise(0, HALVES[0])
                                factors(0, HALVES[0])
                            else:
                                h = k // (PAIRS - 1)
                                stats(i + 1, 0, h)
                                variances(0, HALVES[h])
                        assert at[0] == AHEAD[k], at[0]
                        chain[0], start[0], at[0] = order
                    if k in (PAIRS - 4, PAIRS - 3):
                        with dve.If(i > NB // 2 - 2):
                            low_weights(0, 0, (k - (PAIRS - 4),))
                    if k == PAIRS - 2:
                        with dve.If(i > NB // 2 - 2):
                            normalise_rows(0, 0, 0)
            assert at[0] == BODY, at[0]
            start[0] = before + (NB // 2) * BODY
            at[0] = 0

            v.memset(s1[:, 6, :], 0.0).then_inc(y_free, 2)
            v.memset(s1[:, 7, :], 0.0).then_inc(h_lo_ready, 2)

            def low_xnT(e):
                for c in range(KC):
                    dve.wait_ge(xnT_hi_ready, 2 * e + c + 1)
                    low(xnT_lo[:, c, :], xt_ps[c][:], xnT_hi[:, c, :]).then_inc(xnT_lo_ready, 1)

            def low_hidden(e, n):
                dve.wait_ge(h_hi_ready, HC * e + n + 1)
                low(hT_lo[:, n, :], relu[n % 2][:], hT_hi[:, n, :]).then_inc(h_lo_ready, 1)

            def expert(i, q, last_one=False):
                e = 2 * i + q
                for n in range(HC):
                    low_hidden(e, n)
                    if n == 3 and not last_one:
                        normalise_rows(i + q, 1 - q, e + 1)
                if not last_one:
                    low_xnT(e + 1)
                dve.wait_ge(res_loaded[q], 16 * S * (i + 1))
                dve.wait_ge(b2_loaded[q], 16 * (i + 1))
                for s in range(S):
                    last = v.scalar_tensor_tensor(res[q][:, s, :], b2b[q][:], record(e, s, 3), res[q][:, s, :],
                                                  ALU.mult, ALU.add)
                link(last)
                if not last_one:
                    low_weights(e + 1, 1 - q, range(PIECES))
                banks = 0
                for s in range(S):
                    if s == 0 or y_ends(s - 1, last_one):
                        banks += 1
                        dve.wait_ge(y_done, 2 * e + banks)
                    last = v.scalar_tensor_tensor(res[q][:, s, :], y_tile(s, last_one), record(e, s, 3), res[q][:, s, :],
                                                  ALU.mult, ALU.add)
                    if y_ends(s, last_one):
                        last.then_inc(y_free, 1)
                if not last_one:
                    dve.wait_ge(y_free, 2 * e + 4)
                    v.memset(s1[:, 6, :], 0.0).then_inc(res_ready, 1)

            low_xnT(0)
            low_weights(0, 0, range(PIECES // 2, PIECES))
            for q in range(2):
                dve.wait_ge(o_stored[q], NB // 2 * 32 + 1)
            base = start[0] + at[0]
            at[0] = 0
            with dve.Fori(0, E // 2 - 1) as i:
                start[0] = base + 2 * i
                expert(i, 0)
                expert(i, 1)
            assert at[0] == 2
            start[0] = base + 2 * (E // 2 - 1)
            at[0] = 0
            expert(E // 2 - 1, 0)
            expert(E // 2 - 1, 1, last_one=True)


_INS = ["L0_attn_x", "L0_attn_norm_w", "L0_attn_norm_b", "L0_attn_qkv_w", "L0_attn_qkv_b", "L0_attn_proj_w",
        "L0_attn_proj_b", "L0_ffn_Wg", "L0_ffn_bg", "L0_ffn_W1", "L0_ffn_b1", "L0_ffn_W2", "L0_ffn_b2"]


def kernel(**inputs):
    import numpy as np
    import concourse.bacc as bacc
    from concourse.bass_utils import run_bass_kernel_spmd

    nc = bacc.Bacc("TRN2", target_bir_lowering=False, num_devices=1)
    arrays, args = {}, []
    for name in _INS:
        a = np.ascontiguousarray(inputs[name])
        arrays[f"in_{name}"] = a
        args.append(nc.dram_tensor(f"in_{name}", a.shape, mybir.dt.from_np(a.dtype), kind="ExternalInput").ap())
    out = nc.dram_tensor("out", (NB, T, C), F32, kind="ExternalOutput").ap()
    program(nc, *args, out)
    r = run_bass_kernel_spmd(nc, [arrays], core_ids=[0])
    return r.results[0]["out"]
```
